# Optimizing a Trainium2 kernel written in Bass

```python
import numpy as np
import jax
import jax.numpy as jnp

def _softmax(x, axis=-1):
    return jax.nn.softmax(x, axis=axis)

def _gelu(x):
    return jax.nn.gelu(x, approximate=True)

def _silu(x):
    return jax.nn.silu(x)

def _sigmoid(x):
    return jax.nn.sigmoid(x)

def _layernorm(x, axis=-1, eps=1e-05):
    m = jnp.mean(x, axis=axis, keepdims=True)
    v = jnp.var(x, axis=axis, keepdims=True)
    return (x - m) / jnp.sqrt(v + eps)

def _scatter_add(tgt, idx, src, axis=0):
    return tgt.at[idx].add(src)

def _segment_sum(src, seg, n):
    return jax.ops.segment_sum(src, seg, n)
kernel_name = 'mk_cond_resid_d4_seqx_r2_c711b4'

def setup_inputs(seed: int=0):
    np.random.seed(seed)
    _w = jnp.asarray

    def _rec_inputs():
        import jax
        import jax.numpy as jnp
        _rk = jax.random.key(seed)
        x = -0.0003929 + 0.9999 * jax.random.normal(jax.random.fold_in(_rk, 1), (2, 2048, 512), jnp.float32)
        _lenS = 2048 - jax.random.randint(jax.random.fold_in(_rk, 7), (2,), 0, max(1, 2048 // 4) + 1, jnp.int32)
        _lenS2 = 2048 - jax.random.randint(jax.random.fold_in(_rk, 8), (2,), 0, max(1, 2048 // 4) + 1, jnp.int32)
        itok_B_0_63 = jax.random.randint(jax.random.fold_in(_rk, 11), (2,), 0, 64, jnp.int32)
        itok_B_0_7 = jax.random.randint(jax.random.fold_in(_rk, 12), (2,), 0, 8, jnp.int32)
        itok_B_0_8 = jax.random.randint(jax.random.fold_in(_rk, 13), (2,), 0, 9, jnp.int32)
        itok_B_0_3 = jax.random.randint(jax.random.fold_in(_rk, 14), (2,), 0, 4, jnp.int32)
        return (x, itok_B_0_63, itok_B_0_7, itok_B_0_8, itok_B_0_3)
    x, itok_B_0_63, itok_B_0_7, itok_B_0_8, itok_B_0_3 = _rec_inputs()

    def _L0_cond_setup():
        import jax, jax.numpy as jnp
        import numpy as np
        NUM_CATEGORIES = 64
        INPUT_DIM = 512
        HIDDEN_DIM = 512
        B = 128
        S = 64
        key = jax.random.key(seed)
        kx, kc, kw = jax.random.split(key, 3)
        x = jax.random.normal(kx, (B, S, INPUT_DIM), dtype=jnp.float32)
        cat_ids = jax.random.randint(kc, (B,), 0, NUM_CATEGORIES, dtype=jnp.int32)
        W = 0.02 * jax.random.normal(kw, (NUM_CATEGORIES, INPUT_DIM, HIDDEN_DIM), dtype=jnp.float32)
        b = jnp.zeros((NUM_CATEGORIES, HIDDEN_DIM), dtype=jnp.float32)
        return {'x': x, 'cat_ids': cat_ids, 'W': W, 'b': b}
    _L0_cond_all = _L0_cond_setup()
    _L0_cond_in = {k: v for k, v in _L0_cond_all.items() if k in ('W', 'b')}
    del _L0_cond_all

    def _L1_cond_setup():
        import jax, jax.numpy as jnp
        import numpy as np
        B, S, D, F = (32, 256, 512, 2048)
        R_COMMON, R_DOMAIN, E = (16, 16, 8)
        ALPHA = 2.0

        def _expert_lora(x, expert_ids, Wa, Wb):
            Ab = Wa[expert_ids]
            Bb = Wb[expert_ids]
            low = jnp.einsum('bsd,brd->bsr', x, Ab)
            return ALPHA * jnp.einsum('bsr,bor->bso', low, Bb)
        key = jax.random.key(seed)
        ks = jax.random.split(key, 12)
        sd = lambda k, shape: jax.random.normal(k, shape, dtype=jnp.float32) * (1.0 / np.sqrt(shape[-1]))
        return {'hidden_states': jax.random.normal(ks[0], (B, S, D), dtype=jnp.float32), 'expert_ids': jax.random.randint(ks[1], (B,), 0, E, dtype=jnp.int32), 'wi': sd(ks[2], (F, D)), 'wo': sd(ks[3], (D, F)), 'common_wi_a': sd(ks[4], (R_COMMON, D)), 'common_wi_b': sd(ks[5], (F, R_COMMON)), 'common_wo_a': sd(ks[6], (R_COMMON, F)), 'common_wo_b': sd(ks[7], (D, R_COMMON)), 'experts_wi_a': sd(ks[8], (E, R_DOMAIN, D)), 'experts_wi_b': sd(ks[9], (F, R_DOMAIN)) * jnp.ones((E, 1, 1)) * 0.0 + sd(ks[9], (E, F, R_DOMAIN)), 'experts_wo_a': sd(ks[10], (E, R_DOMAIN, F)), 'experts_wo_b': sd(ks[11], (E, D, R_DOMAIN))}
    _L1_cond_all = _L1_cond_setup()
    _L1_cond_in = {k: v for k, v in _L1_cond_all.items() if k in ('wi', 'wo', 'common_wi_a', 'common_wi_b', 'common_wo_a', 'common_wo_b', 'experts_wi_a', 'experts_wi_b', 'experts_wo_a', 'experts_wo_b')}
    del _L1_cond_all

    def _L2_cond_setup():
        import jax, jax.numpy as jnp
        import numpy as np
        LN_EPS = 1e-05
        key = jax.random.key(seed)
        ks = jax.random.split(key, 8)
        B, S, H, A, L = (32, 1024, 512, 128, 10)
        return {'hidden_states': jax.random.normal(ks[0], (B, S, H), dtype=jnp.float32), 'language_ids': jax.random.randint(ks[1], (B,), 0, L, dtype=jnp.int64), 'W1': jax.random.normal(ks[2], (L, H, A), dtype=jnp.float32) * (1.0 / np.sqrt(H)), 'b1': jnp.zeros((L, A), dtype=jnp.float32), 'W2': jax.random.normal(ks[3], (L, A, H), dtype=jnp.float32) * (1.0 / np.sqrt(A)), 'b2': jnp.zeros((L, H), dtype=jnp.float32), 'gamma': jnp.ones((L, H), dtype=jnp.float32), 'beta': jnp.zeros((L, H), dtype=jnp.float32)}
    _L2_cond_all = _L2_cond_setup()
    _L2_cond_in = {k: v for k, v in _L2_cond_all.items() if k in ('W1', 'b1', 'W2', 'b2', 'gamma', 'beta')}
    del _L2_cond_all

    def _L3_cond_setup():
        import jax, jax.numpy as jnp
        import numpy as np
        D = 512
        RANK = 16
        ALPHA = 16.0
        SCALING = ALPHA / RANK
        N_LANG = 4
        B, S = (32, 1024)
        key = jax.random.key(seed)
        k1, k2, k3, k4, k5 = jax.random.split(key, 5)
        x = jax.random.normal(k1, (B, S, D), dtype=jnp.float32)
        language_ids = jax.random.randint(k2, (B,), 0, N_LANG, dtype=jnp.int32)
        lora_A = jax.random.normal(k3, (N_LANG, RANK, D), dtype=jnp.float32) * 0.02
        lora_B = jax.random.normal(k4, (N_LANG, D, RANK), dtype=jnp.float32) * 0.02
        lang_embed = jax.random.normal(k5, (N_LANG, D), dtype=jnp.float32) * 0.02
        return {'x': x, 'language_ids': language_ids, 'lora_A': lora_A, 'lora_B': lora_B, 'lang_embed': lang_embed}
    _L3_cond_all = _L3_cond_setup()
    _L3_cond_in = {k: v for k, v in _L3_cond_all.items() if k in ('lora_A', 'lora_B', 'lang_embed')}
    del _L3_cond_all
    return {'x': x, 'itok_B_0_63': itok_B_0_63, 'itok_B_0_7': itok_B_0_7, 'itok_B_0_8': itok_B_0_8, 'itok_B_0_3': itok_B_0_3, 'L0_cond_W': _L0_cond_in['W'], 'L0_cond_b': _L0_cond_in['b'], 'L1_cond_wi': _L1_cond_in['wi'], 'L1_cond_wo': _L1_cond_in['wo'], 'L1_cond_common_wi_a': _L1_cond_in['common_wi_a'], 'L1_cond_common_wi_b': _L1_cond_in['common_wi_b'], 'L1_cond_common_wo_a': _L1_cond_in['common_wo_a'], 'L1_cond_common_wo_b': _L1_cond_in['common_wo_b'], 'L1_cond_experts_wi_a': _L1_cond_in['experts_wi_a'], 'L1_cond_experts_wi_b': _L1_cond_in['experts_wi_b'], 'L1_cond_experts_wo_a': _L1_cond_in['experts_wo_a'], 'L1_cond_experts_wo_b': _L1_cond_in['experts_wo_b'], 'L2_cond_W1': _L2_cond_in['W1'], 'L2_cond_b1': _L2_cond_in['b1'], 'L2_cond_W2': _L2_cond_in['W2'], 'L2_cond_b2': _L2_cond_in['b2'], 'L2_cond_gamma': _L2_cond_in['gamma'], 'L2_cond_beta': _L2_cond_in['beta'], 'L3_cond_lora_A': _L3_cond_in['lora_A'], 'L3_cond_lora_B': _L3_cond_in['lora_B'], 'L3_cond_lang_embed': _L3_cond_in['lang_embed']}

def reference(x, itok_B_0_63, itok_B_0_7, itok_B_0_8, itok_B_0_3, L0_cond_W, L0_cond_b, L1_cond_wi, L1_cond_wo, L1_cond_common_wi_a, L1_cond_common_wi_b, L1_cond_common_wo_a, L1_cond_common_wo_b, L1_cond_experts_wi_a, L1_cond_experts_wi_b, L1_cond_experts_wo_a, L1_cond_experts_wo_b, L2_cond_W1, L2_cond_b1, L2_cond_W2, L2_cond_b2, L2_cond_gamma, L2_cond_beta, L3_cond_lora_A, L3_cond_lora_B, L3_cond_lang_embed):
    import jax
    import jax.numpy as jnp

    def _L0_cond_ref(x, cat_ids, W, b):
        import jax, jax.numpy as jnp
        import numpy as np
        NUM_CATEGORIES = 64
        INPUT_DIM = 512
        HIDDEN_DIM = 512
        B = 128
        S = 64
        selected_W = W[cat_ids]
        selected_b = b[cat_ids]
        out = jnp.einsum('bsd,bdh->bsh', x, selected_W) + selected_b[:, None, :]
        return out

    def _L1_cond_ref(hidden_states, expert_ids, wi, wo, common_wi_a, common_wi_b, common_wo_a, common_wo_b, experts_wi_a, experts_wi_b, experts_wo_a, experts_wo_b):
        import jax, jax.numpy as jnp
        import numpy as np
        B, S, D, F = (32, 256, 512, 2048)
        R_COMMON, R_DOMAIN, E = (16, 16, 8)
        ALPHA = 2.0

        def _expert_lora(x, expert_ids, Wa, Wb):
            Ab = Wa[expert_ids]
            Bb = Wb[expert_ids]
            low = jnp.einsum('bsd,brd->bsr', x, Ab)
            return ALPHA * jnp.einsum('bsr,bor->bso', low, Bb)
        x = hidden_states
        hidden_i = jnp.einsum('bsd,fd->bsf', x, wi)
        hidden_i += ALPHA * jnp.einsum('bsr,fr->bsf', jnp.einsum('bsd,rd->bsr', x, common_wi_a), common_wi_b)
        hidden_i += _expert_lora(x, expert_ids, experts_wi_a, experts_wi_b)
        hidden_i = jax.nn.relu(hidden_i)
        hidden_o = jnp.einsum('bsf,df->bsd', hidden_i, wo)
        hidden_o += ALPHA * jnp.einsum('bsr,dr->bsd', jnp.einsum('bsf,rf->bsr', hidden_i, common_wo_a), common_wo_b)
        hidden_o += _expert_lora(hidden_i, expert_ids, experts_wo_a, experts_wo_b)
        return hidden_o

    def _L2_cond_ref(hidden_states, language_ids, W1, b1, W2, b2, gamma, beta):
        import jax, jax.numpy as jnp
        import numpy as np
        LN_EPS = 1e-05
        w1 = W1[language_ids]
        w2 = W2[language_ids]
        h = jnp.einsum('bsh,bha->bsa', hidden_states, w1) + b1[language_ids][:, None, :]
        h = jax.nn.relu(h)
        adapted = jnp.einsum('bsa,bah->bsh', h, w2) + b2[language_ids][:, None, :]
        x = hidden_states + adapted
        mean = jnp.mean(x, axis=-1, keepdims=True)
        var = jnp.mean(jnp.square(x - mean), axis=-1, keepdims=True)
        normed = (x - mean) * jax.lax.rsqrt(var + LN_EPS)
        return normed * gamma[language_ids][:, None, :] + beta[language_ids][:, None, :]

    def _L3_cond_ref(x, language_ids, lora_A, lora_B, lang_embed):
        import jax, jax.numpy as jnp
        import numpy as np
        D = 512
        RANK = 16
        ALPHA = 16.0
        SCALING = ALPHA / RANK
        N_LANG = 4
        B, S = (32, 1024)
        A = lora_A[language_ids]
        Bm = lora_B[language_ids]
        emb = lang_embed[language_ids]
        t = jnp.einsum('bsd,brd->bsr', x, A)
        lora_out = jnp.einsum('bsr,bdr->bsd', t, Bm) * SCALING
        return lora_out + emb[:, None, :]
    x = x + _L0_cond_ref(x, itok_B_0_63, L0_cond_W, L0_cond_b)
    x = x + _L1_cond_ref(x, itok_B_0_7, L1_cond_wi, L1_cond_wo, L1_cond_common_wi_a, L1_cond_common_wi_b, L1_cond_common_wo_a, L1_cond_common_wo_b, L1_cond_experts_wi_a, L1_cond_experts_wi_b, L1_cond_experts_wo_a, L1_cond_experts_wo_b)
    x = x + _L2_cond_ref(x, itok_B_0_8, L2_cond_W1, L2_cond_b1, L2_cond_W2, L2_cond_b2, L2_cond_gamma, L2_cond_beta)
    x = x + _L3_cond_ref(x, itok_B_0_3, L3_cond_lora_A, L3_cond_lora_B, L3_cond_lang_embed)
    return x

_drawn_inputs = setup_inputs


def setup_inputs(seed=0):
    import zlib

    import numpy as np

    out = dict(_drawn_inputs(seed))
    spreads = {'L0_cond_b': (0.0, 0.1),
     'L2_cond_b1': (0.0, 2.0),
     'L2_cond_b2': (0.0, 2.0),
     'L2_cond_gamma': (1.0, 0.6),
     'L2_cond_beta': (0.0, 0.629)}
    factors = {'L3_cond_lang_embed': 23.443}
    for name, (base, spread) in spreads.items():
        noise = np.random.default_rng([zlib.crc32(name.encode()), seed]).standard_normal(out[name].shape)
        drawn = base * np.exp(spread * noise) if base else spread * noise
        out[name] = jnp.asarray(drawn.astype(out[name].dtype))
    for name, factor in factors.items():
        out[name] = (out[name] * factor).astype(out[name].dtype)
    return out
```

```python
from contextlib import ExitStack

import concourse.bass as bass
from concourse import mybir

F32 = mybir.dt.float32
F16 = mybir.dt.float16
I32 = mybir.dt.int32
ALU = mybir.AluOpType
ACT = mybir.ActivationFunctionType

P = 128
D = 512
F = 2048
NB = 2
T = 512
GROUPS = 8
PER_SEQ = GROUPS // NB
DC = D // P
FC = F // P
RANK = 16
R2 = 2 * RANK
R6 = 3 * R2

W0_SCALE = 64.0
HIDDEN_SCALE = 16.0
WO_SCALE = 64.0
LORA_ALPHA = 2.0
WI_B_SCALE = 4.0
WI_A_SCALE = LORA_ALPHA * HIDDEN_SCALE / WI_B_SCALE
WO_B_SCALE = 4.0
WO_A_SCALE = LORA_ALPHA * WO_SCALE / WO_B_SCALE
W1_SCALE = 32.0
W2_SCALE = 16.0
A3_SCALE = 64.0
B3_SCALE = 64.0
LN_EPS = 1e-5

STAGE_SLOTS = 6
HIDDEN_SLOTS = 3
SUM_SLOTS = 2

B2_AT, GAMMA_AT, BETA_AT, B1_AT, VEC2 = 0, DC, 2 * DC, 3 * DC, 3 * DC + 1


def staging_plan():
    plan = {(0, -1): [("W0", 0, k) for k in range(DC)]
            + [("WiA", 0, 0), ("WiB", 0, 0), ("WoB", 0, 0), ("WoA", 0, 0)]
            + [("w", 0, u) for u in range(4)]}
    later = [("W1", 0, 0), ("W2", 0, 0), ("B3", 0, 0)] + [("W0", 1, k) for k in range(DC)]
    later += [("WiA", 1, 0), ("WoB", 1, 0)] + [(n, 1, j) for j in range(4) for n in ("WiB", "WoA")]
    later += [("W1", 1, 0), ("W2", 1, 0), ("B3", 1, 0)]
    for k in range(FC):
        plan[0, k] = []
        if k in (1, 5, 9):
            plan[0, k] += [("WiB", 0, k // 4 + 1), ("WoA", 0, k // 4 + 1)]
        elif k > 1:
            plan[0, k] += later[:2]
            later = later[2:]
        if k < FC - 2:
            plan[0, k] += [("w", 0, 2 * k + 4), ("w", 0, 2 * k + 5)]
    assert not later
    plan[PER_SEQ, -1] = [("w", 1, u) for u in range(4)]
    for k in range(FC - 2):
        plan[PER_SEQ, k] = [("w", 1, 2 * k + 4), ("w", 1, 2 * k + 5)]
    return plan


def build(nc, x, ids, w0, b0, wi, wo, wi_a, wi_b, wo_a, wo_b, w1, w2, vec2, a3, b3, emb, out):
    plan = staging_plan()
    order = [item for place in plan.values() for item in place]
    at = {item: n for n, item in enumerate(order)}
    plain = [item for item in order if item[0] != "w"]
    plain_at = {item: n for n, item in enumerate(plain)}

    ctx = ExitStack()
    with ctx:
        def sb(name, shape, dt=F32):
            return ctx.enter_context(nc.sbuf_tensor(name, shape, dt))

        def sem(name):
            return ctx.enter_context(nc.semaphore(name))

        wi_h, wi_l = (sb(f"wi_{p}", [P, FC, DC, P], F16) for p in "hl")
        wo_h, wo_l = (sb(f"wo_{p}", [P, FC, D], F16) for p in "hl")
        w0_h, w0_l = (sb(f"w0_{p}", [P, NB, DC, D], F16) for p in "hl")
        w1_h, w1_l = (sb(f"w1_{p}", [P, NB, DC, P], F16) for p in "hl")
        w2_h, w2_l = (sb(f"w2_{p}", [P, NB, D], F16) for p in "hl")
        wi_a_s = sb("wi_a_s", [R6, NB, D], F16)
        wi_b_s = sb("wi_b_s", [R6, NB, F], F16)
        wo_a_s = sb("wo_a_s", [R6, NB, F], F16)
        wo_b_s = sb("wo_b_s", [R6, NB, D], F16)
        a3_s = sb("a3_s", [P, NB, DC, R2], F16)
        b3_s = sb("b3_s", [R6, NB, D], F16)
        stage = sb("stage", [P, STAGE_SLOTS, D])
        wsum = sb("wsum", [P, SUM_SLOTS, D])
        x_in = sb("x_in", [P, DC, T])
        x_h, x_l = (sb(f"x_{p}", [P, DC, T], F16) for p in "hl")
        x1 = sb("x1", [P, DC, T])
        x1_h, x1_l = (sb(f"x1_{p}", [P, DC, T], F16) for p in "hl")
        hid_h, hid_l = (sb(f"hid_{p}", [P, HIDDEN_SLOTS, T], F16) for p in "hl")
        x2 = sb("x2", [P, DC, T])
        x23_h, x23_l = (sb(f"x23_{p}", [P, DC, T], F16) for p in "hl")
        y = sb("y", [P, DC, T])
        o = sb("o", [P, DC, T])
        up_h, up_l = (sb(f"up_{p}", [P, T], F16) for p in "hl")
        total = sb("total", [P, T])
        up = total
        total_h, total_l = (sb(f"total_{p}", [P, T], F16) for p in "hl")
        rstd = sb("rstd", [P, T])
        low_s = sb("low_s", [R6, T], F16)
        b0_s = sb("b0_s", [P, NB, DC])
        vec2_s = sb("vec2_s", [P, NB, VEC2])
        emb_s = sb("emb_s", [P, NB, DC])
        a3_in = sb("a3_in", [P, NB, DC, RANK])
        ids_s = sb("ids_s", [1, 4 * NB], I32)
        ident = sb("ident", [P, P])
        ones = sb("ones", [P, P], F16)
        eps = sb("eps", [P, 1])

        acc = [ctx.enter_context(nc.psum_tensor(f"acc{m}", [P, T], F32)) for m in range(DC)]
        hid = [ctx.enter_context(nc.psum_tensor(f"hid{m}", [P, T], F32)) for m in range(2)]
        side = ctx.enter_context(nc.psum_tensor("side", [P, T], F32))
        merge = ctx.enter_context(nc.psum_tensor("merge", [P, T], F32))
        l0_bank = [hid[0], hid[1], side, hid[0]]

        small_in = sem("small_in")
        x_loaded = sem("x_loaded")
        stage_in = [sem(f"stage_in{n}") for n in range(STAGE_SLOTS)]
        stored = sem("stored")
        l0_done = sem("l0_done")
        hid_done = sem("hid_done")
        chunk_done = sem("chunk_done")
        up_done = sem("up_done")
        down_done = sem("down_done")
        stat_done = sem("stat_done")
        low_done = sem("low_done")
        lora_done = sem("lora_done")
        merge_done = sem("merge_done")
        x_high = sem("x_high")
        x1_full = sem("x1_full")
        hid_high = sem("hid_high")
        x2_high = sem("x2_high")
        up_full = sem("up_full")
        adapted = sem("adapted")
        total_high = sem("total_high")
        squared = sem("squared")
        std_done = sem("std_done")
        scaled = sem("scaled")
        x3_high = sem("x3_high")
        low_high = sem("low_high")
        out_biased = sem("out_biased")
        plain_high = sem("plain_high")
        a3_high = sem("a3_high")
        merged_high = sem("merged_high")
        eye_added = sem("eye_added")
        tile_done = sem("tile_done")
        a3_low = sem("a3_low")
        x_low = sem("x_low")
        x1_high = sem("x1_high")
        x1_low = sem("x1_low")
        hid_low = sem("hid_low")
        x2_full = sem("x2_full")
        x2_low = sem("x2_low")
        up_low = sem("up_low")
        y_full = sem("y_full")
        summed = sem("summed")
        total_low = sem("total_low")
        centred = sem("centred")
        rstd_done = sem("rstd_done")
        normed = sem("normed")
        x3_full = sem("x3_full")
        x3_low = sem("x3_low")
        low_low = sem("low_low")
        out_ready = sem("out_ready")
        const_set = sem("const_set")
        merged_low = sem("merged_low")

        block = ctx.enter_context(nc.Block())

        def plain_tile(item):
            name, b, k = item
            t = slice(k * D, (k + 1) * D)
            src = stage[:, at[item] % STAGE_SLOTS, :]
            if name == "W0":
                return W0_SCALE, src, w0_h[:, b, k, :], w0_l[:, b, k, :], slice(0, P)
            if name == "W1":
                flat = (w[:, b].rearrange("p c a -> p (c a)") for w in (w1_h, w1_l))
                return (W1_SCALE, src, *flat, slice(0, P))
            if name == "W2":
                return W2_SCALE, src, w2_h[:, b, :], w2_l[:, b, :], slice(0, P)
            dst, scale, first = {
                "WiA": (wi_a_s[:, b, :], WI_A_SCALE, 2 * R2), "WiB": (wi_b_s[:, b, t], WI_B_SCALE, R2),
                "WoA": (wo_a_s[:, b, t], WO_A_SCALE, 2 * R2), "WoB": (wo_b_s[:, b, :], WO_B_SCALE, R2),
                "B3": (b3_s[:, b, :], B3_SCALE, 2 * R2)}[name]
            return scale, src[0:R6], dst, dst, slice(first, first + R2)

        @block.sync
        def _(sp):
            sp.dma_start(ids_s[:, :], ids[:, :]).then_inc(stored, 16)
            sp.dma_start(x_in[:, :, :], x[0]).then_inc(x_loaded, 16)
            sp.wait_ge(stored, 16)
            most = (w0.shape[0], wi_a.shape[0], w1.shape[0], a3.shape[0])
            cat, expert, language, lora = (
                [sp.value_load(ids_s[0:1, NB * n + b:NB * n + b + 1], min_val=0, max_val=most[n] - 1)
                 for b in range(NB)] for n in range(4))

            def load_stage(item):
                name, b, k = item
                t = slice(k * D, (k + 1) * D)
                n = at[item]
                slot = n % STAGE_SLOTS
                rows = P
                if name == "w":
                    src = wi[k // 2] if k % 2 == 0 else wo[k // 2]
                elif name == "W0":
                    src = w0[cat[b], k * P:(k + 1) * P, :]
                elif name == "W1":
                    src = w1[language[b]]
                elif name == "W2":
                    src = w2[language[b]]
                else:
                    rows = R6
                    src = {"WiA": lambda: wi_a[expert[b]], "WiB": lambda: wi_b[expert[b], :, t],
                           "WoA": lambda: wo_a[expert[b], :, t], "WoB": lambda: wo_b[expert[b]],
                           "B3": lambda: b3[lora[b]]}[name]()
                if n >= STAGE_SLOTS:
                    sp.wait_ge(tile_done, n - STAGE_SLOTS + 1)
                sp.dma_start(stage[0:rows, slot, :], src).then_inc(stage_in[slot], 16)

            def load_x(s):
                sp.wait_ge(x_low, DC * s)
                sp.dma_start(x_in[:, :, :], x[s]).then_inc(x_loaded, 16)

            def store(t):
                for m in range(DC):
                    sp.wait_ge(out_ready, DC * t + m + 1)
                    sp.dma_start(out[t, :, m, :], o[:, m, :]).then_inc(stored, 16)

            for item in plan[0, -1][:DC]:
                load_stage(item)
            for b in range(NB):
                sp.dma_start(b0_s[:, b, :], b0[cat[b]]).then_inc(small_in, 16)
                sp.dma_start(vec2_s[:, b, :], vec2[language[b]]).then_inc(small_in, 16)
                sp.dma_start(emb_s[:, b, :], emb[lora[b]]).then_inc(small_in, 16)
                sp.dma_start(a3_in[:, b, :, :], a3[lora[b]]).then_inc(small_in, 16)
            for item in plan[0, -1][DC:]:
                load_stage(item)
            load_x(1)
            for k in range(FC):
                for item in plan[0, k]:
                    load_stage(item)
            with sp.Fori(1, PER_SEQ) as s:
                load_x(s + 1)
                store(s - 1)
            for k in range(-1, FC - 2):
                for item in plan[PER_SEQ, k]:
                    load_stage(item)
            load_x(PER_SEQ + 1)
            store(PER_SEQ - 1)
            with sp.Fori(PER_SEQ + 1, GROUPS - 1) as s:
                load_x(s + 1)
                store(s - 1)
            store(GROUPS - 2)
            store(GROUPS - 1)
            sp.wait_ge(stored, 16 + 16 * DC * GROUPS)

        @block.gpsimd
        def _(pool):
            pool.memset(ident[:, :], 0.0).then_inc(const_set, 1)
            pool.memset(ones[:, :], 1.0 / D).then_inc(const_set, 1)
            pool.memset(eps[:, :], LN_EPS).then_inc(const_set, 1)
            pool.wait_ge(const_set, 1)
            pool.affine_select(out=ident[:, :], in_=ident[:, :], compare_op=ALU.not_equal, fill=1.0,
                               base=0, pattern=[[-1, P]], channel_multiplier=1).then_inc(const_set, 1)
            for item in order:
                if item[0] == "w":
                    _, b, u = item
                    n = 2 * FC * b + u
                    pool.wait_ge(merged_high, n + 1)
                    src = wsum[:, n % SUM_SLOTS, :]
                    high, low = ((w[:, u // 2].rearrange("p c f -> p (c f)") if u % 2 == 0 else v[:, u // 2, :])
                                 for w, v in ((wi_h, wo_h), (wi_l, wo_l)))
                    pool.tensor_tensor(low, src, high, ALU.subtract).then_inc(merged_low, 1)

        @block.tensor
        def _(pe):
            def three(dst, weights, data, first=True, last=True):
                (wh, wl), (xh, xl) = weights, data
                pe.matmul(dst, wh, xh, start=first, stop=False)
                pe.matmul(dst, wh, xl, start=False, stop=False)
                return pe.matmul(dst, wl, xh, start=False, stop=last)

            def merge_lora(b, u):
                k = u // 2
                if (b, u) != (0, 0):
                    last_unit = ("w", b, u - 1) if u else ("w", b - 1, 2 * FC - 1)
                    pe.wait_ge(tile_done, at[last_unit] + 1)
                part = k * P // D
                for item in ([("WiA", b, 0), ("WiB", b, part)] if u % 2 == 0 else [("WoA", b, part), ("WoB", b, 0)]):
                    pe.wait_ge(tile_done, at[item] + 1)
                f = slice(k * P, (k + 1) * P)
                if u % 2 == 0:
                    for c in range(DC):
                        d = slice(c * P, (c + 1) * P)
                        last = pe.matmul(merge[:, d], wi_a_s[:, b, d], wi_b_s[:, b, f], start=True, stop=True)
                else:
                    last = pe.matmul(merge[:, :], wo_a_s[:, b, f], wo_b_s[:, b, :], start=True, stop=True)
                last.then_inc(merge_done, 1)

            def layer0(s, b, m, tail):
                if m == 0:
                    pe.wait_ge(x_high, DC * s + DC)
                    pe.wait_ge(x_low, DC * s + DC)
                    pe.wait_ge(tile_done, at["W0", b, DC - 1] + 1)
                    if tail:
                        pe.wait_ge(hid_low, FC * s)
                if m == 3:
                    pe.wait_ge(x1_full, DC * s + 1)
                d = slice(m * P, (m + 1) * P)
                for c in range(DC):
                    last = three(l0_bank[m][:, :], (w0_h[:, b, c, d], w0_l[:, b, c, d]),
                                 (x_h[:, c, :], x_l[:, c, :]), c == 0, c == DC - 1)
                last.then_inc(l0_done, 1)

            def adapter_up(t, b, drained):
                pe.wait_ge(x2_high, DC * t + DC)
                pe.wait_ge(x2_low, DC * t + DC)
                pe.wait_ge(tile_done, at["W1", b, 0] + 1)
                pe.wait_ge(*drained)
                for c in range(DC):
                    last = three(side[:, :], (w1_h[:, b, c, :], w1_l[:, b, c, :]),
                                 (x23_h[:, c, :], x23_l[:, c, :]), c == 0, c == DC - 1)
                last.then_inc(up_done, 1)

            def adapter_down(t, b, m):
                if m == 0:
                    pe.wait_ge(up_full, 2 * t + 2)
                    pe.wait_ge(up_low, t + 1)
                    pe.wait_ge(tile_done, at["W2", b, 0] + 1)
                else:
                    pe.wait_ge(adapted, DC * t + m)
                d = slice(m * P, (m + 1) * P)
                three(side[:, :], (w2_h[:, b, d], w2_l[:, b, d]), (up_h[:, :], up_l[:, :])).then_inc(down_done, 1)

            def statistic(t, n):
                pe.wait_ge(total_low, 2 * t + n + 1)
                pe.matmul(side[:, :], ones[:, :], total_h[:, :], start=True, stop=False)
                pe.matmul(side[:, :], ones[:, :], total_l[:, :], start=False, stop=True).then_inc(stat_done, 1)

            def lora_low(t, b):
                pe.wait_ge(x3_high, DC * t + DC)
                pe.wait_ge(x3_low, DC * t + DC)
                pe.wait_ge(a3_low, b + 1)
                for c in range(DC):
                    pe.matmul(side[0:R2, :], a3_s[:, b, c, :], x23_h[:, c, :], start=c == 0, stop=False)
                    last = pe.matmul(side[0:R2, :], a3_s[:, b, c, :], x23_l[:, c, :], start=False, stop=c == DC - 1)
                last.then_inc(low_done, 1)

            def lora_up(t, b, m):
                if m == 0:
                    pe.wait_ge(low_high, 2 * t + 2)
                    pe.wait_ge(low_low, t + 1)
                    pe.wait_ge(tile_done, at["B3", b, 0] + 1)
                else:
                    pe.wait_ge(out_biased, DC * t + m)
                d = slice(m * P, (m + 1) * P)
                pe.matmul(side[:, :], b3_s[:, b, d], low_s[:, :], start=True, stop=True).then_inc(lora_done, 1)

            def first_product(s, b, k, prep):
                if k == 0:
                    pe.wait_ge(x1_low, DC * s + DC)
                elif k >= 2:
                    pe.wait_ge(hid_low, FC * s + k - 1)
                if prep:
                    pe.wait_ge(merged_low, 2 * FC * b + 2 * k + 1)
                for c in range(DC):
                    last = three(hid[k % 2][:, :], (wi_h[:, k, c, :], wi_l[:, k, c, :]),
                                 (x1_h[:, c, :], x1_l[:, c, :]), c == 0, c == DC - 1)
                last.then_inc(hid_done, 1)

            def second_product(s, b, k, prep, tail):
                pe.wait_ge(hid_low, FC * s + k + 1)
                if k == 0 and tail:
                    pe.wait_ge(x2_full, DC * s)
                if prep:
                    pe.wait_ge(merged_low, 2 * FC * b + 2 * k + 2)
                slot = k % HIDDEN_SLOTS
                for m in range(DC):
                    d = slice(m * P, (m + 1) * P)
                    last = three(acc[m][:, :], (wo_h[:, k, d], wo_l[:, k, d]),
                                 (hid_h[:, slot, :], hid_l[:, slot, :]), k == 0, k == FC - 1)
                last.then_inc(chunk_done, 1)

            def step(s, b, prep, tail, tail_b):
                for m in range(DC):
                    layer0(s, b, m, tail)
                    if prep:
                        merge_lora(b, m)
                if tail:
                    adapter_up(s - 1, tail_b, (x1_full, DC * s + 3))
                for k in range(FC + 2):
                    if k < FC:
                        first_product(s, b, k, prep)
                    if prep and k < FC - 2:
                        merge_lora(b, 2 * k + 4)
                    if tail:
                        if k in (1, 2, 3):
                            adapter_down(s - 1, tail_b, (0, 1, 3)[k - 1])
                        if k == 11:
                            lora_low(s - 1, tail_b)
                        if k in (12, 13):
                            lora_up(s - 1, tail_b, 2 * (k - 12))
                    if k >= 2:
                        second_product(s, b, k - 2, prep, tail)
                    if prep and k < FC - 2:
                        merge_lora(b, 2 * k + 5)
                    if tail:
                        if k == 2:
                            adapter_down(s - 1, tail_b, 2)
                        if k in (4, 7):
                            statistic(s - 1, (k - 4) // 3)
                        if k in (12, 13):
                            lora_up(s - 1, tail_b, 2 * (k - 12) + 1)

            pe.wait_ge(const_set, 4)
            step(0, 0, True, False, None)
            with pe.Fori(1, PER_SEQ) as s:
                step(s, 0, False, True, 0)
            step(PER_SEQ, 1, True, True, 0)
            with pe.Fori(PER_SEQ + 1, GROUPS) as s:
                step(s, 1, False, True, 1)
            t, b = GROUPS - 1, NB - 1
            adapter_up(t, b, (out_biased, DC * t))
            for m in range(DC):
                adapter_down(t, b, m)
            statistic(t, 0)
            statistic(t, 1)
            lora_low(t, b)
            for m in range(DC):
                lora_up(t, b, m)

        @block.scalar
        def _(act):
            def high_plain(item):
                n = at[item]
                if item[0] == "W0":
                    act.wait_ge(eye_added, DC * item[1] + item[2] + 1)
                else:
                    act.wait_ge(stage_in[n % STAGE_SLOTS], 16 * (n // STAGE_SLOTS + 1))
                scale, src, high, _, _ = plain_tile(item)
                act.activation(high, src, ACT.Copy, scale=scale).then_inc(plain_high, 1)

            def high_a3(b):
                act.wait_ge(small_in, 16 * 4 * NB)
                act.activation(a3_s[:, b, :, 0:RANK], a3_in[:, b, :, :], ACT.Copy, scale=A3_SCALE)\
                    .then_inc(a3_high, 1)

            def high_merged(b, u):
                n = 2 * FC * b + u
                act.wait_ge(tile_done, at["w", b, u] + 1)
                high = wi_h[:, u // 2].rearrange("p c f -> p (c f)") if u % 2 == 0 else wo_h[:, u // 2, :]
                act.activation(high, wsum[:, n % SUM_SLOTS, :], ACT.Copy).then_inc(merged_high, 1)

            def split_x(s):
                act.wait_ge(x_loaded, 16 * s + 16)
                for c in range(DC):
                    act.activation(x_h[:, c, :], x_in[:, c, :], ACT.Copy).then_inc(x_high, 1)

            def high_x2(t):
                for m in range(DC):
                    act.wait_ge(x2_full, DC * t + m + 1)
                    act.activation(x23_h[:, m, :], x2[:, m, :], ACT.Copy).then_inc(x2_high, 1)

            def leave_layer0(s, b, m):
                act.wait_ge(l0_done, DC * s + m + 1)
                act.activation(x1[:, m, :], l0_bank[m][:, :], ACT.Identity, bias=b0_s[:, b, m:m + 1],
                               scale=1.0 / W0_SCALE).then_inc(x1_full, 1)

            def adapter_relu(t, b):
                act.wait_ge(up_done, t + 1)
                for dst in (up, up_h):
                    act.activation(dst[:, :], side[:, :], ACT.Relu, bias=vec2_s[:, b, B1_AT:B1_AT + 1],
                                   scale=1.0 / W1_SCALE).then_inc(up_full, 1)

            def high_hidden(s, k, later):
                act.wait_ge(hid_done, FC * s + k + 1)
                if later or k >= HIDDEN_SLOTS:
                    act.wait_ge(chunk_done, FC * s + k - HIDDEN_SLOTS + 1)
                act.activation(hid_h[:, k % HIDDEN_SLOTS, :], hid[k % 2][:, :], ACT.Relu).then_inc(hid_high, 1)

            def leave_adapter(t, b, m):
                act.wait_ge(down_done, DC * t + m + 1)
                act.activation(y[:, m, :], side[:, :], ACT.Identity, bias=vec2_s[:, b, B2_AT + m:B2_AT + m + 1],
                               scale=1.0 / W2_SCALE).then_inc(adapted, 1)

            def high_total(t, n):
                act.wait_ge(summed, 6 * t + 3 * n + 3)
                act.activation(total_h[:, :], total[:, :], ACT.Copy).then_inc(total_high, 1)

            def square(t):
                act.wait_ge(stored, 16 + 16 * DC * t)
                for m in range(DC):
                    act.wait_ge(centred, DC * t + m + 1)
                    act.activation(o[:, m, :], y[:, m, :], ACT.Square).then_inc(squared, 1)

            def std(t):
                act.wait_ge(stat_done, 2 * t + 2)
                act.activation(rstd[:, :], side[:, :], ACT.Sqrt, bias=eps[:, :]).then_inc(std_done, 1)

            def scale_and_shift(t, b):
                for m in range(DC):
                    act.wait_ge(normed, DC * t + m + 1)
                    act.activation(y[:, m, :], y[:, m, :], ACT.Identity,
                                   bias=vec2_s[:, b, BETA_AT + m:BETA_AT + m + 1],
                                   scale=vec2_s[:, b, GAMMA_AT + m:GAMMA_AT + m + 1]).then_inc(scaled, 1)

            def high_x3(t):
                for m in range(DC):
                    act.wait_ge(x3_full, DC * t + m + 1)
                    act.activation(x23_h[:, m, :], y[:, m, :], ACT.Copy).then_inc(x3_high, 1)

            def high_low_rank(t):
                act.wait_ge(low_done, t + 1)
                for first in (0, 2 * R2):
                    act.activation(low_s[first:first + R2, :], side[0:R2, :], ACT.Copy).then_inc(low_high, 1)

            def leave_lora(t, b, m):
                act.wait_ge(lora_done, DC * t + m + 1)
                act.activation(o[:, m, :], side[:, :], ACT.Identity, bias=emb_s[:, b, m:m + 1],
                               scale=1.0 / (A3_SCALE * B3_SCALE)).then_inc(out_biased, 1)

            def staged(place):
                for item in plan.get(place, []):
                    if item[0] == "w":
                        high_merged(item[1], item[2])
                    else:
                        if item[0] == "B3":
                            high_a3(item[1])
                        high_plain(item)

            def step(s, b, prep, tail, tail_b, more):
                if tail:
                    high_x2(s - 1)
                for m in range(DC):
                    leave_layer0(s, b, m)
                    if prep:
                        high_merged(b, m)
                if tail:
                    adapter_relu(s - 1, tail_b)
                for k in range(FC):
                    high_hidden(s, k, tail)
                    if prep:
                        staged((PER_SEQ * b, k))
                    if tail:
                        if k == 1:
                            leave_adapter(s - 1, tail_b, 0)
                        if k == 2:
                            leave_adapter(s - 1, tail_b, 1)
                            leave_adapter(s - 1, tail_b, 2)
                        if k == 3:
                            leave_adapter(s - 1, tail_b, 3)
                        if k in (4, 7):
                            high_total(s - 1, (k - 4) // 3)
                        if k == 5:
                            square(s - 1)
                        if k == 8:
                            std(s - 1)
                        if k == 9:
                            scale_and_shift(s - 1, tail_b)
                        if k == 10:
                            high_x3(s - 1)
                        if k == 11:
                            high_low_rank(s - 1)
                        if k in (12, 13):
                            leave_lora(s - 1, tail_b, 2 * (k - 12))
                            leave_lora(s - 1, tail_b, 2 * (k - 12) + 1)
                    if k == 14 and more:
                        split_x(s + 1)

            act.wait_ge(small_in, 16 * 4 * NB)
            act.wait_ge(const_set, 4)
            split_x(0)
            for item in plan[0, -1][:2 * DC]:
                high_plain(item)
            step(0, 0, True, False, None, True)
            with act.Fori(1, PER_SEQ) as s:
                step(s, 0, False, True, 0, True)
            step(PER_SEQ, 1, True, True, 0, True)
            with act.Fori(PER_SEQ + 1, GROUPS - 1) as s:
                step(s, 1, False, True, 1, True)
            step(GROUPS - 1, 1, False, True, 1, False)
            t, b = GROUPS - 1, NB - 1
            high_x2(t)
            adapter_relu(t, b)
            for m in range(DC):
                leave_adapter(t, b, m)
            high_total(t, 0)
            square(t)
            high_total(t, 1)
            std(t)
            scale_and_shift(t, b)
            high_x3(t)
            high_low_rank(t)
            for m in range(DC):
                leave_lora(t, b, m)

        @block.vector
        def _(dve):
            def add_eye(item):
                _, b, c = item
                n = at[item]
                dve.wait_ge(stage_in[n % STAGE_SLOTS], 16 * (n // STAGE_SLOTS + 1))
                part = stage[:, n % STAGE_SLOTS, c * P:(c + 1) * P]
                dve.tensor_tensor(part, part, ident[:, :], ALU.add).then_inc(eye_added, 1)

            def low_plain(item):
                dve.wait_ge(plain_high, plain_at[item] + 1)
                scale, src, high, low, rows = plain_tile(item)
                dve.scalar_tensor_tensor(low[rows], src[rows], scale, high[rows], ALU.mult, ALU.subtract)\
                    .then_inc(tile_done, 1)

            def low_a3(b):
                dve.wait_ge(a3_high, b + 1)
                dve.scalar_tensor_tensor(a3_s[:, b, :, RANK:R2], a3_in[:, b, :, :], A3_SCALE, a3_s[:, b, :, 0:RANK],
                                         ALU.mult, ALU.subtract).then_inc(a3_low, 1)

            def sum_unit(b, u):
                n = 2 * FC * b + u
                slot = at["w", b, u]
                dve.wait_ge(stage_in[slot % STAGE_SLOTS], 16 * (slot // STAGE_SLOTS + 1))
                dve.wait_ge(merge_done, n + 1)
                if n >= SUM_SLOTS:
                    dve.wait_ge(merged_low, n - SUM_SLOTS + 1)
                dve.scalar_tensor_tensor(wsum[:, n % SUM_SLOTS, :], stage[:, slot % STAGE_SLOTS, :],
                                         HIDDEN_SCALE if u % 2 == 0 else WO_SCALE, merge[:, :],
                                         ALU.mult, ALU.add).then_inc(tile_done, 1)

            def split_x(s):
                for c in range(DC):
                    dve.wait_ge(x_high, DC * s + c + 1)
                    dve.tensor_tensor(x_l[:, c, :], x_in[:, c, :], x_h[:, c, :], ALU.subtract).then_inc(x_low, 1)

            def leave_layer1(t, m):
                dve.wait_ge(chunk_done, FC * t + FC)
                dve.scalar_tensor_tensor(x2[:, m, :], acc[m][:, :], 1.0 / (HIDDEN_SCALE * WO_SCALE), x1[:, m, :],
                                         ALU.mult, ALU.add).then_inc(x2_full, 1)

            def low_x2(t, m):
                dve.wait_ge(x2_high, DC * t + m + 1)
                dve.tensor_tensor(x23_l[:, m, :], x2[:, m, :], x23_h[:, m, :], ALU.subtract).then_inc(x2_low, 1)

            def split_x1(s, m):
                dve.wait_ge(x1_full, DC * s + m + 1)
                dve.tensor_copy(x1_h[:, m, :], x1[:, m, :]).then_inc(x1_high, 1)
                dve.wait_ge(x1_high, DC * s + m + 1)
                dve.tensor_tensor(x1_l[:, m, :], x1[:, m, :], x1_h[:, m, :], ALU.subtract).then_inc(x1_low, 1)

            def low_hidden(s, k):
                dve.wait_ge(hid_high, FC * s + k + 1)
                dve.scalar_tensor_tensor(hid_l[:, k % HIDDEN_SLOTS, :], hid[k % 2][:, :], 0.0,
                                         hid_h[:, k % HIDDEN_SLOTS, :], ALU.max, ALU.subtract).then_inc(hid_low, 1)

            def adapter_low(t):
                dve.wait_ge(up_full, 2 * t + 2)
                dve.tensor_tensor(up_l[:, :], up[:, :], up_h[:, :], ALU.subtract).then_inc(up_low, 1)

            def add_x2(t, m):
                dve.wait_ge(adapted, DC * t + m + 1)
                dve.tensor_tensor(y[:, m, :], y[:, m, :], x2[:, m, :], ALU.add).then_inc(y_full, 1)

            def add_chunks(t, n, src, ready):
                dve.wait_ge(ready, DC * t + 2)
                dve.tensor_tensor(total[:, :], src[:, 0, :], src[:, 1, :], ALU.add).then_inc(summed, 1)
                for m in (2, 3):
                    dve.wait_ge(ready, DC * t + m + 1)
                    dve.wait_ge(summed, 6 * t + 3 * n + m - 1)
                    dve.tensor_tensor(total[:, :], total[:, :], src[:, m, :], ALU.add).then_inc(summed, 1)

            def low_total(t, n):
                dve.wait_ge(total_high, 2 * t + n + 1)
                dve.tensor_tensor(total_l[:, :], total[:, :], total_h[:, :], ALU.subtract).then_inc(total_low, 1)

            def centre(t):
                dve.wait_ge(stat_done, 2 * t + 1)
                for m in range(DC):
                    dve.tensor_tensor(y[:, m, :], y[:, m, :], side[:, :], ALU.subtract).then_inc(centred, 1)

            def normalise(t):
                dve.wait_ge(std_done, t + 1)
                dve.reciprocal(rstd[:, :], rstd[:, :]).then_inc(rstd_done, 1)
                dve.wait_ge(rstd_done, t + 1)
                for m in range(DC):
                    dve.tensor_tensor(y[:, m, :], y[:, m, :], rstd[:, :], ALU.mult).then_inc(normed, 1)

            def add_x3(t):
                for m in range(DC):
                    dve.wait_ge(scaled, DC * t + m + 1)
                    dve.tensor_tensor(y[:, m, :], y[:, m, :], x2[:, m, :], ALU.add).then_inc(x3_full, 1)

            def low_x3(t):
                for m in range(DC):
                    dve.wait_ge(x3_high, DC * t + m + 1)
                    dve.tensor_tensor(x23_l[:, m, :], y[:, m, :], x23_h[:, m, :], ALU.subtract).then_inc(x3_low, 1)

            def low_low_rank(t):
                dve.wait_ge(low_high, 2 * t + 2)
                dve.tensor_tensor(low_s[R2:2 * R2, :], side[0:R2, :], low_s[0:R2, :], ALU.subtract)\
                    .then_inc(low_low, 1)

            def add_out(t, m):
                dve.wait_ge(out_biased, DC * t + m + 1)
                dve.tensor_tensor(o[:, m, :], o[:, m, :], y[:, m, :], ALU.add).then_inc(out_ready, 1)

            def staged(place):
                for item in plan.get(place, []):
                    if item[0] == "w":
                        sum_unit(item[1], item[2])
                    else:
                        if item[0] == "W0":
                            add_eye(item)
                        if item[0] == "B3":
                            low_a3(item[1])
                        low_plain(item)

            def step(s, b, prep, tail, more):
                t = s - 1
                if tail:
                    for m in range(DC):
                        leave_layer1(t, m)
                for m in range(DC):
                    if prep:
                        sum_unit(b, m)
                    if tail:
                        low_x2(t, m)
                    split_x1(s, m)
                for k in range(FC):
                    low_hidden(s, k)
                    if prep:
                        staged((PER_SEQ * b, k))
                    if tail:
                        if k == 0:
                            adapter_low(t)
                        if k == 2:
                            add_x2(t, 0)
                            add_x2(t, 1)
                        if k == 3:
                            add_x2(t, 2)
                            add_x2(t, 3)
                            add_chunks(t, 0, y, y_full)
                        if k in (4, 7):
                            low_total(t, (k - 4) // 3)
                        if k == 5:
                            centre(t)
                        if k == 6:
                            add_chunks(t, 1, o, squared)
                        if k == 8:
                            normalise(t)
                        if k == 9:
                            add_x3(t)
                        if k == 10:
                            low_x3(t)
                        if k == 11:
                            low_low_rank(t)
                        if k == 12:
                            add_out(t, 0)
                        if k == 13:
                            add_out(t, 1)
                            add_out(t, 2)
                        if k == 14:
                            add_out(t, 3)
                    if k == 14 and more:
                        split_x(s + 1)

            dve.wait_ge(const_set, 4)
            for item in plan[0, -1][:DC]:
                add_eye(item)
            split_x(0)
            for item in plan[0, -1][:2 * DC]:
                low_plain(item)
            step(0, 0, True, False, True)
            with dve.Fori(1, PER_SEQ) as s:
                step(s, 0, False, True, True)
            step(PER_SEQ, 1, True, True, True)
            with dve.Fori(PER_SEQ + 1, GROUPS - 1) as s:
                step(s, 1, False, True, True)
            step(GROUPS - 1, 1, False, True, False)
            t = GROUPS - 1
            for m in range(DC):
                leave_layer1(t, m)
            for m in range(DC):
                low_x2(t, m)
            adapter_low(t)
            for m in range(DC):
                add_x2(t, m)
            add_chunks(t, 0, y, y_full)
            low_total(t, 0)
            centre(t)
            add_chunks(t, 1, o, squared)
            low_total(t, 1)
            normalise(t)
            add_x3(t)
            low_x3(t)
            low_low_rank(t)
            for m in range(DC):
                add_out(t, m)


def kernel(x, itok_B_0_63, itok_B_0_7, itok_B_0_8, itok_B_0_3, L0_cond_W, L0_cond_b, L1_cond_wi, L1_cond_wo,
           L1_cond_common_wi_a, L1_cond_common_wi_b, L1_cond_common_wo_a, L1_cond_common_wo_b,
           L1_cond_experts_wi_a, L1_cond_experts_wi_b, L1_cond_experts_wo_a, L1_cond_experts_wo_b,
           L2_cond_W1, L2_cond_b1, L2_cond_W2, L2_cond_b2, L2_cond_gamma, L2_cond_beta,
           L3_cond_lora_A, L3_cond_lora_B, L3_cond_lang_embed):
    import numpy as np
    from concourse import bacc
    from concourse.bass_utils import run_bass_kernel_spmd

    def lay(a, *order):
        return np.ascontiguousarray(np.transpose(a, order))

    def stacked(common, experts):
        both = [np.concatenate([common, e], axis=0) for e in experts]
        return np.ascontiguousarray(np.stack([np.concatenate([v] * 3, axis=0) for v in both]))

    def columns(v):
        return np.asarray(v).reshape(-1, DC, P).transpose(0, 2, 1)

    x, wi, wo = (np.asarray(v) for v in (x, L1_cond_wi, L1_cond_wo))
    ea, eb, oa, ob = (np.asarray(v) for v in (L1_cond_experts_wi_a, L1_cond_experts_wi_b,
                                              L1_cond_experts_wo_a, L1_cond_experts_wo_b))
    arrays = {
        "x": lay(x.reshape(GROUPS, T, DC, P), 0, 3, 2, 1),
        "ids": np.ascontiguousarray(np.concatenate([np.asarray(v) for v in (
            itok_B_0_63, itok_B_0_7, itok_B_0_8, itok_B_0_3)]).reshape(1, 4 * NB)),
        "w0": np.ascontiguousarray(L0_cond_W),
        "b0": np.ascontiguousarray(columns(L0_cond_b)),
        "wi": lay(wi.reshape(FC, P, DC, P), 0, 3, 2, 1).reshape(FC, P, D),
        "wo": lay(wo, 1, 0).reshape(FC, P, D),
        "wi_a": stacked(np.asarray(L1_cond_common_wi_a), ea),
        "wi_b": stacked(np.asarray(L1_cond_common_wi_b).T, eb.transpose(0, 2, 1)),
        "wo_a": stacked(np.asarray(L1_cond_common_wo_a), oa),
        "wo_b": stacked(np.asarray(L1_cond_common_wo_b).T, ob.transpose(0, 2, 1)),
        "w1": lay(np.asarray(L2_cond_W1).reshape(-1, DC, P, P), 0, 2, 1, 3).reshape(-1, P, D),
        "w2": np.ascontiguousarray(L2_cond_W2),
        "vec2": np.ascontiguousarray(np.concatenate(
            [columns(L2_cond_b2), columns(L2_cond_gamma), columns(L2_cond_beta),
             np.asarray(L2_cond_b1)[:, :, None]], axis=2)),
        "a3": lay(np.asarray(L3_cond_lora_A).reshape(-1, RANK, DC, P), 0, 3, 2, 1),
        "b3": np.ascontiguousarray(np.concatenate([np.asarray(L3_cond_lora_B).transpose(0, 2, 1)] * 6, axis=1)),
        "emb": np.ascontiguousarray(columns(L3_cond_lang_embed)),
    }
    nc = bacc.Bacc("TRN2", target_bir_lowering=False, num_devices=1)
    args = [nc.dram_tensor(name, a.shape, mybir.dt.from_np(a.dtype), kind="ExternalInput").ap()
            for name, a in arrays.items()]
    out = nc.dram_tensor("out", (GROUPS, P, DC, T), F32, kind="ExternalOutput").ap()
    build(nc, *args, out)
    r = run_bass_kernel_spmd(nc, [arrays], core_ids=[0])
    return r.results[0]["out"].transpose(0, 3, 2, 1).reshape(x.shape)
```

```python
from contextlib import ExitStack

import concourse.bass as bass
from concourse import mybir

F32 = mybir.dt.float32
F16 = mybir.dt.float16
I32 = mybir.dt.int32
ALU = mybir.AluOpType
ACT = mybir.ActivationFunctionType

P = 128
D = 512
F = 2048
NB = 2
T = 512
GROUPS = 8
PASSES = GROUPS + 1
HALF = T // 2
QUARTER = T // 4
PER_SEQ = GROUPS // NB
DC = D // P
FC = F // P
RANK = 16
R2 = 2 * RANK
R6 = 3 * R2

W0_SCALE = 64.0
HIDDEN_SCALE = 16.0
WO_SCALE = 64.0
LORA_ALPHA = 2.0
WI_B_SCALE = 4.0
WI_A_SCALE = LORA_ALPHA * HIDDEN_SCALE / WI_B_SCALE
WO_B_SCALE = 4.0
WO_A_SCALE = LORA_ALPHA * WO_SCALE / WO_B_SCALE
W1_SCALE = 32.0
W2_SCALE = 16.0
A3_SCALE = 64.0
B3_SCALE = 64.0
LN_EPS = 1e-5

STAGE_SLOTS = 6
HIDDEN_SLOTS = 3
SUM_SLOTS = 2
WARM_UPS = 20

SMALL_LOADS = 16 * (4 * NB - 1)

B2_AT, GAMMA_AT, BETA_AT, B1_AT, VEC2 = 0, DC, 2 * DC, 3 * DC, 3 * DC + 1


def staging_plan():
    plan = {(0, -1): [("W0", 0, k) for k in range(DC)]
            + [("WiA", 0, 0), ("WiB", 0, 0), ("WoB", 0, 0), ("WoA", 0, 0)]
            + [("w", 0, u) for u in range(4)]}
    later = [("W1", 0, 0), ("W2", 0, 0), ("B3", 0, 0)] + [("W0", 1, k) for k in range(DC)]
    later += [("WiA", 1, 0), ("WoB", 1, 0)] + [(n, 1, j) for j in range(4) for n in ("WiB", "WoA")]
    later += [("W1", 1, 0), ("W2", 1, 0), ("B3", 1, 0)]
    for k in range(FC):
        plan[0, k] = [("w", 0, 2 * k + 4), ("w", 0, 2 * k + 5)] if k < FC - 2 else []
        if k in (0, 4, 8):
            plan[0, k] += [("WiB", 0, k // 4 + 1), ("WoA", 0, k // 4 + 1)]
        elif k > 1:
            plan[0, k] += later[:2]
            later = later[2:]
    assert not later
    plan[PER_SEQ, -1] = [("w", 1, u) for u in range(4)]
    for k in range(FC - 2):
        plan[PER_SEQ, k] = [("w", 1, 2 * k + 4), ("w", 1, 2 * k + 5)]
    return plan


def build(nc, x, ids, w0, b0, wi, wo, wi_a, wi_b, wo_a, wo_b, w1, w2, vec2, a3, b3, emb, out):
    plan = staging_plan()
    order = [item for place in plan.values() for item in place]
    at = {item: n for n, item in enumerate(order)}
    plain = [item for item in order if item[0] != "w"]
    plain_at = {item: n for n, item in enumerate(plain)}

    ctx = ExitStack()
    with ctx:
        def sb(name, shape, dt=F32):
            return ctx.enter_context(nc.sbuf_tensor(name, shape, dt))

        def sem(name):
            return ctx.enter_context(nc.semaphore(name))

        wi_h, wi_l = (sb(f"wi_{p}", [P, FC, DC, P], F16) for p in "hl")
        wo_h, wo_l = (sb(f"wo_{p}", [P, FC, D], F16) for p in "hl")
        w0_h, w0_l = (sb(f"w0_{p}", [P, NB, DC, D], F16) for p in "hl")
        w1_h, w1_l = (sb(f"w1_{p}", [P, NB, DC, P], F16) for p in "hl")
        w2_h, w2_l = (sb(f"w2_{p}", [P, NB, D], F16) for p in "hl")
        wi_a_s = sb("wi_a_s", [R6, NB, D], F16)
        wi_b_s = sb("wi_b_s", [R6, NB, F], F16)
        wo_a_s = sb("wo_a_s", [R6, NB, F], F16)
        wo_b_s = sb("wo_b_s", [R6, NB, D], F16)
        a3_s = sb("a3_s", [P, NB, DC, R2], F16)
        b3_s = sb("b3_s", [R6, NB, D], F16)
        stage = sb("stage", [P, STAGE_SLOTS, D])
        wsum = sb("wsum", [P, SUM_SLOTS, D])
        x_in = sb("x_in", [P, DC, T])
        x_h, x_l = (sb(f"x_{p}", [P, DC, T], F16) for p in "hl")
        x1 = sb("x1", [P, DC, T])
        x1_h, x1_l = (sb(f"x1_{p}", [P, DC, T], F16) for p in "hl")
        hid_h, hid_l = (sb(f"hid_{p}", [P, HIDDEN_SLOTS, T], F16) for p in "hl")
        x2 = sb("x2", [P, DC, T])
        x23_h, x23_l = (sb(f"x23_{p}", [P, DC, T], F16) for p in "hl")
        y = sb("y", [P, DC, T])
        o = sb("o", [P, DC, T])
        up_h, up_l = (sb(f"up_{p}", [P, T], F16) for p in "hl")
        total = sb("total", [P, T])
        up = total
        total_h, total_l = (sb(f"total_{p}", [P, T], F16) for p in "hl")
        rstd = sb("rstd", [P, T])
        low_s = sb("low_s", [R6, T], F16)
        b0_s = sb("b0_s", [P, NB, DC])
        vec2_s = sb("vec2_s", [P, NB, VEC2])
        emb_s = sb("emb_s", [P, NB, DC])
        a3_in = sb("a3_in", [P, NB, DC, RANK])
        ids_s = sb("ids_s", [1, 4 * NB], I32)
        ident = sb("ident", [P, P])
        ones = sb("ones", [P, P], F16)
        eps = sb("eps", [P, 1])

        acc = [ctx.enter_context(nc.psum_tensor(f"acc{m}", [P, T], F32)) for m in range(DC)]
        hid = [ctx.enter_context(nc.psum_tensor(f"hid{m}", [P, T], F32)) for m in range(2)]
        side = ctx.enter_context(nc.psum_tensor("side", [P, T], F32))
        merge = ctx.enter_context(nc.psum_tensor("merge", [P, T], F32))
        l0_bank = [hid[0], hid[1], hid[0], hid[1]]

        whole = (slice(0, T), side, [side])
        half = (slice(0, HALF), side, [side])
        parts = [(slice(0, QUARTER), hid[0], [acc[0], acc[1], side]),
                 (slice(QUARTER, HALF), hid[1], [acc[2], acc[3], merge])]

        def merge_bank(b, u):
            return side if b == 0 and u % 2 else merge

        b0_in = sem("b0_in")
        small_in = sem("small_in")
        x0_in = [sem(f"x0_in{c}") for c in range(DC)]
        x_loaded = sem("x_loaded")
        stage_in = [sem(f"stage_in{n}") for n in range(STAGE_SLOTS)]
        stored = sem("stored")
        l0_done = sem("l0_done")
        hid_done = sem("hid_done")
        chunk_done = sem("chunk_done")
        acc_done = sem("acc_done")
        up_done = sem("up_done")
        down_done = sem("down_done")
        stat_done = [sem(f"stat_done{n}") for n in range(2)]
        low_done = sem("low_done")
        lora_done = sem("lora_done")
        merge_done = sem("merge_done")
        x_high = sem("x_high")
        x1_full = sem("x1_full")
        hid_high = sem("hid_high")
        x2_high = sem("x2_high")
        up_full = sem("up_full")
        adapted = sem("adapted")
        total_high = [sem(f"total_high{n}") for n in range(2)]
        squared = sem("squared")
        std_done = sem("std_done")
        scaled = sem("scaled")
        x3_high = sem("x3_high")
        low_high = sem("low_high")
        out_biased = sem("out_biased")
        plain_high = sem("plain_high")
        a3_high = sem("a3_high")
        merged_high = sem("merged_high")
        eye_added = sem("eye_added")
        tile_done = sem("tile_done")
        a3_low = sem("a3_low")
        x_low = sem("x_low")
        x1_high = sem("x1_high")
        x1_low = sem("x1_low")
        hid_low = sem("hid_low")
        x2_full = sem("x2_full")
        x2_low = sem("x2_low")
        up_low = sem("up_low")
        y_full = sem("y_full")
        summed = [sem(f"summed{n}") for n in range(2)]
        total_low = [sem(f"total_low{n}") for n in range(2)]
        centred = sem("centred")
        rstd_done = sem("rstd_done")
        normed = sem("normed")
        x3_full = sem("x3_full")
        x3_low = sem("x3_low")
        low_low = sem("low_low")
        out_ready = sem("out_ready")
        const_set = sem("const_set")
        warm_set = sem("warm_set")
        merged_low = sem("merged_low")

        block = ctx.enter_context(nc.Block())

        def plain_tile(item):
            name, b, k = item
            t = slice(k * D, (k + 1) * D)
            src = stage[:, at[item] % STAGE_SLOTS, :]
            if name == "W0":
                return W0_SCALE, src, w0_h[:, b, k, :], w0_l[:, b, k, :], slice(0, P)
            if name == "W1":
                flat = (w[:, b].rearrange("p c a -> p (c a)") for w in (w1_h, w1_l))
                return (W1_SCALE, src, *flat, slice(0, P))
            if name == "W2":
                return W2_SCALE, src, w2_h[:, b, :], w2_l[:, b, :], slice(0, P)
            dst, scale, first = {
                "WiA": (wi_a_s[:, b, :], WI_A_SCALE, 2 * R2), "WiB": (wi_b_s[:, b, t], WI_B_SCALE, R2),
                "WoA": (wo_a_s[:, b, t], WO_A_SCALE, 2 * R2), "WoB": (wo_b_s[:, b, :], WO_B_SCALE, R2),
                "B3": (b3_s[:, b, :], B3_SCALE, 2 * R2)}[name]
            return scale, src[0:R6], dst, dst, slice(first, first + R2)

        @block.sync
        def _(sp):
            sp.dma_start(ids_s[:, :], ids[:, :]).then_inc(stored, 16)
            for c in range(2):
                sp.dma_start(x_in[:, c, :], x[0, :, c, :]).then_inc(x0_in[c], 16)
            sp.wait_ge(stored, 16)

            def chosen(n, rows):
                return [sp.value_load(ids_s[0:1, NB * n + b:NB * n + b + 1], min_val=0, max_val=rows - 1)
                        for b in range(NB)]

            cat = chosen(0, w0.shape[0])

            def load_stage(item):
                name, b, k = item
                t = slice(k * D, (k + 1) * D)
                n = at[item]
                slot = n % STAGE_SLOTS
                rows = P
                if name == "w":
                    src = wi[k // 2] if k % 2 == 0 else wo[k // 2]
                elif name == "W0":
                    src = w0[cat[b], k * P:(k + 1) * P, :]
                elif name == "W1":
                    src = w1[language[b]]
                elif name == "W2":
                    src = w2[language[b]]
                else:
                    rows = R6
                    src = {"WiA": lambda: wi_a[expert[b]], "WiB": lambda: wi_b[expert[b], :, t],
                           "WoA": lambda: wo_a[expert[b], :, t], "WoB": lambda: wo_b[expert[b]],
                           "B3": lambda: b3[lora[b]]}[name]()
                if n >= STAGE_SLOTS:
                    sp.wait_ge(tile_done, n - STAGE_SLOTS + 1)
                sp.dma_start(stage[0:rows, slot, :], src).then_inc(stage_in[slot], 16)

            def load_x(s):
                sp.wait_ge(x_low, DC * s)
                sp.dma_start(x_in[:, :, :], x[s]).then_inc(x_loaded, 16)

            def store(t, group, first, where):
                cols = where[0]
                for m in range(DC):
                    sp.wait_ge(out_ready, DC * t + m + 1)
                    sp.dma_start(out[group, :, m, first:first + cols.stop - cols.start], o[:, m, cols])\
                        .then_inc(stored, 16)

            for item in plan[0, -1][:DC]:
                load_stage(item)
                if item[2] < 2:
                    c = item[2] + 2
                    sp.dma_start(x_in[:, c, :], x[0, :, c, :]).then_inc(x0_in[c], 16)
            sp.dma_start(b0_s[:, 0, :], b0[cat[0]]).then_inc(b0_in, 16)
            expert = chosen(1, wi_a.shape[0])
            for item in plan[0, -1][DC:]:
                load_stage(item)
            language = chosen(2, w1.shape[0])
            lora = chosen(3, a3.shape[0])
            sp.dma_start(b0_s[:, 1, :], b0[cat[1]]).then_inc(small_in, 16)
            for b in range(NB):
                sp.dma_start(vec2_s[:, b, :], vec2[language[b]]).then_inc(small_in, 16)
                sp.dma_start(emb_s[:, b, :], emb[lora[b]]).then_inc(small_in, 16)
                sp.dma_start(a3_in[:, b, :, :], a3[lora[b]]).then_inc(small_in, 16)
            for k in range(FC):
                for item in plan[0, k]:
                    load_stage(item)
                if k == 3:
                    load_x(1)
            with sp.Fori(1, PER_SEQ) as s:
                load_x(s + 1)
                store(s - 1, s - 1, 0, whole)
            for k in range(-1, FC - 2):
                for item in plan[PER_SEQ, k]:
                    load_stage(item)
            load_x(PER_SEQ + 1)
            store(PER_SEQ - 1, PER_SEQ - 1, 0, whole)
            with sp.Fori(PER_SEQ + 1, GROUPS - 1) as s:
                load_x(s + 1)
                store(s - 1, s - 1, 0, whole)
            store(GROUPS - 2, GROUPS - 2, 0, whole)
            store(GROUPS - 1, GROUPS - 1, 0, half)
            for h in range(2):
                store(GROUPS + h, GROUPS - 1, HALF + h * QUARTER, parts[h])
            sp.wait_ge(stored, 16 + 16 * DC * (PASSES + 1))

        @block.gpsimd
        def _(pool):
            pool.memset(ident[:, :], 0.0).then_inc(const_set, 1)
            pool.memset(ones[:, :], 1.0 / D).then_inc(const_set, 1)
            pool.memset(eps[:, :], LN_EPS).then_inc(const_set, 1)
            pool.wait_ge(const_set, 1)
            pool.affine_select(out=ident[:, :], in_=ident[:, :], compare_op=ALU.not_equal, fill=1.0,
                               base=0, pattern=[[-1, P]], channel_multiplier=1).then_inc(const_set, 1)
            for item in order:
                if item[0] == "w":
                    _, b, u = item
                    n = 2 * FC * b + u
                    pool.wait_ge(merged_high, n + 1)
                    src = wsum[:, n % SUM_SLOTS, :]
                    high, low = ((w[:, u // 2].rearrange("p c f -> p (c f)") if u % 2 == 0 else v[:, u // 2, :])
                                 for w, v in ((wi_h, wo_h), (wi_l, wo_l)))
                    pool.tensor_tensor(low, src, high, ALU.subtract).then_inc(merged_low, 1)

        @block.tensor
        def _(pe):
            def three(dst, weights, data, first=True, last=True):
                (wh, wl), (xh, xl) = weights, data
                pe.matmul(dst, wh, xh, start=first, stop=False)
                pe.matmul(dst, wh, xl, start=False, stop=False)
                return pe.matmul(dst, wl, xh, start=False, stop=last)

            def merge_lora(b, u):
                k = u // 2
                before = ("w", b, u - 2 + b)
                if before in at:
                    pe.wait_ge(tile_done, at[before] + 1)
                bank = merge_bank(b, u)
                part = k * P // D
                for item in ([("WiA", b, 0), ("WiB", b, part)] if u % 2 == 0 else [("WoA", b, part), ("WoB", b, 0)]):
                    pe.wait_ge(tile_done, at[item] + 1)
                f = slice(k * P, (k + 1) * P)
                if u % 2 == 0:
                    for c in range(DC):
                        d = slice(c * P, (c + 1) * P)
                        last = pe.matmul(bank[:, d], wi_a_s[:, b, d], wi_b_s[:, b, f], start=True, stop=True)
                else:
                    last = pe.matmul(bank[:, :], wo_a_s[:, b, f], wo_b_s[:, b, :], start=True, stop=True)
                last.then_inc(merge_done, 1)

            def layer0(s, b, m, cols, x_pass, x_cols):
                if m == 0:
                    pe.wait_ge(x_high, DC * x_pass + DC)
                    pe.wait_ge(x_low, DC * x_pass + DC)
                    pe.wait_ge(tile_done, at["W0", b, DC - 1] + 1)
                    pe.wait_ge(hid_low, FC * s)
                if m >= 2:
                    pe.wait_ge(x1_full, DC * s + m - 1)
                d = slice(m * P, (m + 1) * P)
                for c in range(DC):
                    last = three(l0_bank[m][:, cols], (w0_h[:, b, c, d], w0_l[:, b, c, d]),
                                 (x_h[:, c, x_cols], x_l[:, c, x_cols]), c == 0, c == DC - 1)
                last.then_inc(l0_done, 1)

            def first_layer0(b):
                for c in range(DC):
                    pe.wait_ge(x_high, c + 1)
                    pe.wait_ge(x_low, c + 1)
                    pe.wait_ge(tile_done, at["W0", b, c] + 1)
                    for m in range(DC):
                        d = slice(m * P, (m + 1) * P)
                        last = three(acc[m][:, :], (w0_h[:, b, c, d], w0_l[:, b, c, d]),
                                     (x_h[:, c, :], x_l[:, c, :]), c == 0, c == DC - 1)
                        if c == DC - 1:
                            last.then_inc(l0_done, 1)
                    if c == DC - 2:
                        merge_lora(b, 0)
                merge_lora(b, 1)
                merge_lora(b, 2)

            def adapter_up(t, b, where):
                pe.wait_ge(x2_high, DC * t + DC)
                pe.wait_ge(x2_low, DC * t + DC)
                pe.wait_ge(tile_done, at["W1", b, 0] + 1)
                cols, bank = where[:2]
                for c in range(DC):
                    last = three(bank[:, cols], (w1_h[:, b, c, :], w1_l[:, b, c, :]),
                                 (x23_h[:, c, cols], x23_l[:, c, cols]), c == 0, c == DC - 1)
                last.then_inc(up_done, 1)

            def adapter_down(t, b, m, where):
                if m == 0:
                    pe.wait_ge(up_full, 2 * t + 2)
                    pe.wait_ge(up_low, t + 1)
                    pe.wait_ge(tile_done, at["W2", b, 0] + 1)
                if m >= len(where[2]):
                    pe.wait_ge(adapted, DC * t + m - len(where[2]) + 1)
                d = slice(m * P, (m + 1) * P)
                cols, bank = where[0], where[2][m % len(where[2])]
                three(bank[:, cols], (w2_h[:, b, d], w2_l[:, b, d]), (up_h[:, cols], up_l[:, cols]))\
                    .then_inc(down_done, 1)

            def statistic(t, n, where):
                pe.wait_ge(total_low[n], t + 1)
                cols, bank = where[:2]
                pe.matmul(bank[:, cols], ones[:, :], total_h[:, cols], start=True, stop=False)
                pe.matmul(bank[:, cols], ones[:, :], total_l[:, cols], start=False, stop=True).then_inc(stat_done[n], 1)

            def lora_low(t, b, where):
                pe.wait_ge(x3_high, DC * t + DC)
                pe.wait_ge(x3_low, DC * t + DC)
                pe.wait_ge(a3_low, b + 1)
                cols, bank = where[:2]
                for c in range(DC):
                    pe.matmul(bank[0:R2, cols], a3_s[:, b, c, :], x23_h[:, c, cols], start=c == 0, stop=False)
                    last = pe.matmul(bank[0:R2, cols], a3_s[:, b, c, :], x23_l[:, c, cols], start=False,
                                     stop=c == DC - 1)
                last.then_inc(low_done, 1)

            def lora_up(t, b, m, where):
                if m == 0:
                    pe.wait_ge(low_high, 2 * t + 2)
                    pe.wait_ge(low_low, t + 1)
                    pe.wait_ge(tile_done, at["B3", b, 0] + 1)
                if m >= len(where[2]):
                    pe.wait_ge(out_biased, DC * t + m - len(where[2]) + 1)
                d = slice(m * P, (m + 1) * P)
                cols, bank = where[0], where[2][m % len(where[2])]
                pe.matmul(bank[:, cols], b3_s[:, b, d], low_s[:, cols], start=True, stop=True)\
                    .then_inc(lora_done, 1)

            def first_product(s, b, k, cols, prep):
                if k == 0:
                    pe.wait_ge(x1_low, DC * s + DC)
                elif k >= 2:
                    pe.wait_ge(hid_low, FC * s + k - 1)
                if prep:
                    pe.wait_ge(merged_low, 2 * FC * b + 2 * k + 1)
                for c in range(DC):
                    last = three(hid[k % 2][:, cols], (wi_h[:, k, c, :], wi_l[:, k, c, :]),
                                 (x1_h[:, c, cols], x1_l[:, c, cols]), c == 0, c == DC - 1)
                last.then_inc(hid_done, 1)

            def second_product(s, b, k, cols, prep, tail):
                pe.wait_ge(hid_low, FC * s + k + 1)
                if k == 0 and tail:
                    pe.wait_ge(x2_full, DC * s)
                if prep:
                    pe.wait_ge(merged_low, 2 * FC * b + 2 * k + 2)
                slot = k % HIDDEN_SLOTS
                for m in range(DC):
                    d = slice(m * P, (m + 1) * P)
                    last = three(acc[m][:, cols], (wo_h[:, k, d], wo_l[:, k, d]),
                                 (hid_h[:, slot, cols], hid_l[:, slot, cols]), k == 0, k == FC - 1)
                    if k == FC - 1:
                        last.then_inc(acc_done, 1)
                if k < FC - 1:
                    last.then_inc(chunk_done, 1)

            def step(s, b, prep, tail=None, tail_b=None, cols=whole[0], x_pass=None, x_cols=whole[0]):
                t = s - 1
                if tail:
                    for m in range(DC):
                        layer0(s, b, m, cols, s if x_pass is None else x_pass, x_cols)
                        if prep:
                            merge_lora(b, m)
                    adapter_up(t, tail_b, tail)
                else:
                    first_layer0(b)
                for k in range(FC + 2):
                    if k < FC:
                        first_product(s, b, k, cols, prep)
                    if k == 0 and not tail:
                        merge_lora(b, 3)
                    if prep and k < FC - 2:
                        merge_lora(b, 2 * k + 4)
                    if tail:
                        if k in (1, 2, 3):
                            adapter_down(t, tail_b, (0, 1, 3)[k - 1], tail)
                        if k in (5, 8):
                            statistic(t, (k - 5) // 3, tail)
                        if k == 13:
                            lora_low(t, tail_b, tail)
                        if k in (14, 15):
                            lora_up(t, tail_b, 2 * (k - 14), tail)
                    if k >= 2:
                        second_product(s, b, k - 2, cols, prep, tail)
                    if prep and k < FC - 2:
                        merge_lora(b, 2 * k + 5)
                    if tail:
                        if k == 2:
                            adapter_down(t, tail_b, 2, tail)
                        if k in (14, 15):
                            lora_up(t, tail_b, 2 * (k - 14) + 1, tail)

            pe.wait_ge(warm_set, 1)
            with pe.Fori(0, WARM_UPS // 4):
                for _ in range(4):
                    pe.matmul(side[:, :], hid_h[:, 0, 0:P], hid_h[:, 0, :], start=True, stop=True)
            pe.wait_ge(const_set, 4)
            step(0, 0, True)
            with pe.Fori(1, PER_SEQ) as s:
                step(s, 0, False, whole, 0)
            step(PER_SEQ, 1, True, whole, 0)
            with pe.Fori(PER_SEQ + 1, GROUPS - 1) as s:
                step(s, 1, False, whole, 1)
            step(GROUPS - 1, 1, False, whole, 1, half[0], GROUPS - 1, half[0])
            step(GROUPS, 1, False, half, 1, half[0], GROUPS - 1, slice(HALF, T))
            t, b = PASSES - 1, NB - 1
            for h in range(2):
                adapter_up(t + h, b, parts[h])
            for h in range(2):
                for m in range(DC):
                    adapter_down(t + h, b, m, parts[h])
            for n in range(2):
                for h in range(2):
                    statistic(t + h, n, parts[h])
            for h in range(2):
                lora_low(t + h, b, parts[h])
            for h in range(2):
                for m in range(DC):
                    lora_up(t + h, b, m, parts[h])

        @block.scalar
        def _(act):
            def high_plain(item):
                n = at[item]
                if item[0] == "W0":
                    act.wait_ge(eye_added, DC * item[1] + item[2] + 1)
                else:
                    act.wait_ge(stage_in[n % STAGE_SLOTS], 16 * (n // STAGE_SLOTS + 1))
                scale, src, high, _, _ = plain_tile(item)
                act.activation(high, src, ACT.Copy, scale=scale).then_inc(plain_high, 1)

            def high_a3(b):
                act.wait_ge(small_in, SMALL_LOADS)
                act.activation(a3_s[:, b, :, 0:RANK], a3_in[:, b, :, :], ACT.Copy, scale=A3_SCALE)\
                    .then_inc(a3_high, 1)

            def high_merged(b, u):
                n = 2 * FC * b + u
                act.wait_ge(tile_done, at["w", b, u] + 1)
                high = wi_h[:, u // 2].rearrange("p c f -> p (c f)") if u % 2 == 0 else wo_h[:, u // 2, :]
                act.activation(high, wsum[:, n % SUM_SLOTS, :], ACT.Copy).then_inc(merged_high, 1)

            def split_x(s):
                act.wait_ge(x_loaded, 16 * s)
                for c in range(DC):
                    act.activation(x_h[:, c, :], x_in[:, c, :], ACT.Copy).then_inc(x_high, 1)

            def high_x2(t, where):
                cols = where[0]
                for m in range(DC):
                    act.wait_ge(x2_full, DC * t + m + 1)
                    act.activation(x23_h[:, m, cols], x2[:, m, cols], ACT.Copy).then_inc(x2_high, 1)

            def leave_layer0(s, b, m, banks, cols):
                act.wait_ge(l0_done, DC * s + m + 1)
                act.activation(x1[:, m, cols], banks[m][:, cols], ACT.Identity, bias=b0_s[:, b, m:m + 1],
                               scale=1.0 / W0_SCALE).then_inc(x1_full, 1)

            def adapter_relu(t, b, where):
                act.wait_ge(up_done, t + 1)
                cols, bank = where[:2]
                for dst in (up, up_h):
                    act.activation(dst[:, cols], bank[:, cols], ACT.Relu, bias=vec2_s[:, b, B1_AT:B1_AT + 1],
                                   scale=1.0 / W1_SCALE).then_inc(up_full, 1)

            def high_hidden(s, k, cols):
                act.wait_ge(hid_done, FC * s + k + 1)
                if k >= HIDDEN_SLOTS:
                    act.wait_ge(chunk_done, (FC - 1) * s + k - HIDDEN_SLOTS + 1)
                act.activation(hid_h[:, k % HIDDEN_SLOTS, cols], hid[k % 2][:, cols], ACT.Relu).then_inc(hid_high, 1)

            def leave_adapter(t, b, m, where):
                act.wait_ge(down_done, DC * t + m + 1)
                cols, bank = where[0], where[2][m % len(where[2])]
                act.activation(y[:, m, cols], bank[:, cols], ACT.Identity, bias=vec2_s[:, b, B2_AT + m:B2_AT + m + 1],
                               scale=1.0 / W2_SCALE).then_inc(adapted, 1)

            def high_total(t, n, where):
                cols = where[0]
                act.wait_ge(summed[n], 3 * t + 3)
                act.activation(total_h[:, cols], total[:, cols], ACT.Copy).then_inc(total_high[n], 1)

            def square(t, group, where):
                cols = where[0]
                act.wait_ge(stored, 16 + 16 * DC * group)
                for m in range(DC):
                    act.wait_ge(centred, DC * t + m + 1)
                    act.activation(o[:, m, cols], y[:, m, cols], ACT.Square).then_inc(squared, 1)

            def std(t, where):
                cols, bank = where[:2]
                act.wait_ge(stat_done[1], t + 1)
                act.activation(rstd[:, cols], bank[:, cols], ACT.Sqrt, bias=eps[:, :]).then_inc(std_done, 1)

            def scale_and_shift(t, b, where):
                cols = where[0]
                for m in range(DC):
                    act.wait_ge(normed, DC * t + m + 1)
                    act.activation(y[:, m, cols], y[:, m, cols], ACT.Identity,
                                   bias=vec2_s[:, b, BETA_AT + m:BETA_AT + m + 1],
                                   scale=vec2_s[:, b, GAMMA_AT + m:GAMMA_AT + m + 1]).then_inc(scaled, 1)

            def high_x3(t, where):
                cols = where[0]
                for m in range(DC):
                    act.wait_ge(x3_full, DC * t + m + 1)
                    act.activation(x23_h[:, m, cols], y[:, m, cols], ACT.Copy).then_inc(x3_high, 1)

            def high_low_rank(t, where):
                cols, bank = where[:2]
                act.wait_ge(low_done, t + 1)
                for first in (0, 2 * R2):
                    act.activation(low_s[first:first + R2, cols], bank[0:R2, cols], ACT.Copy).then_inc(low_high, 1)

            def leave_lora(t, b, m, where):
                cols, bank = where[0], where[2][m % len(where[2])]
                act.wait_ge(lora_done, DC * t + m + 1)
                act.activation(o[:, m, cols], bank[:, cols], ACT.Identity, bias=emb_s[:, b, m:m + 1],
                               scale=1.0 / (A3_SCALE * B3_SCALE)).then_inc(out_biased, 1)

            def plain(b, k):
                for item in plan[PER_SEQ * b, k]:
                    if item[0] == "B3":
                        high_a3(item[1])
                    if item[0] != "w":
                        high_plain(item)

            def step(s, b, prep, tail=None, tail_b=None, cols=whole[0], more=True):
                t = s - 1
                if tail:
                    high_x2(t, tail)
                    for m in range(DC):
                        leave_layer0(s, b, m, l0_bank, cols)
                        if prep:
                            high_merged(b, m)
                    adapter_relu(t, tail_b, tail)
                else:
                    high_merged(b, 0)
                    for m in range(DC):
                        leave_layer0(s, b, m, acc, cols)
                    high_merged(b, 1)
                    high_merged(b, 2)
                for k in range(FC):
                    high_hidden(s, k, cols)
                    if k == 0 and not tail:
                        high_merged(b, 3)
                    if prep and k < FC - 2:
                        high_merged(b, 2 * k + 4)
                    if tail:
                        if k in (1, 2, 3):
                            leave_adapter(t, tail_b, (0, 1, 3)[k - 1], tail)
                        if k in (3, 6):
                            high_total(t, (k - 3) // 3, tail)
                        if k == 5:
                            square(t, t, tail)
                        if k == 8:
                            std(t, tail)
                        if k == 9:
                            scale_and_shift(t, tail_b, tail)
                        if k == 10:
                            high_x3(t, tail)
                        if k == 13:
                            high_low_rank(t, tail)
                        if k in (14, 15):
                            leave_lora(t, tail_b, 2 * (k - 14), tail)
                    if prep and k < FC - 2:
                        high_merged(b, 2 * k + 5)
                    if tail:
                        if k == 2:
                            leave_adapter(t, tail_b, 2, tail)
                        if k in (14, 15):
                            leave_lora(t, tail_b, 2 * (k - 14) + 1, tail)
                    if prep and (PER_SEQ * b, k) in plan:
                        plain(b, k)
                    if k == 13 and more:
                        split_x(s + 1)

            for c, item in enumerate(plan[0, -1][:DC]):
                act.wait_ge(x0_in[c], 16)
                act.activation(x_h[:, c, :], x_in[:, c, :], ACT.Copy).then_inc(x_high, 1)
                high_plain(item)
            for item in plan[0, -1][DC:2 * DC]:
                high_plain(item)
            act.wait_ge(b0_in, 16)
            act.wait_ge(const_set, 4)
            step(0, 0, True)
            act.wait_ge(small_in, SMALL_LOADS)
            with act.Fori(1, PER_SEQ) as s:
                step(s, 0, False, whole, 0)
            step(PER_SEQ, 1, True, whole, 0)
            with act.Fori(PER_SEQ + 1, GROUPS - 1) as s:
                step(s, 1, False, whole, 1)
            step(GROUPS - 1, 1, False, whole, 1, half[0], False)
            step(GROUPS, 1, False, half, 1, half[0], False)
            t, b = PASSES - 1, NB - 1
            for h in range(2):
                high_x2(t + h, parts[h])
            for h in range(2):
                adapter_relu(t + h, b, parts[h])
            for h in range(2):
                for m in range(DC):
                    leave_adapter(t + h, b, m, parts[h])
            for h in range(2):
                high_total(t + h, 0, parts[h])
            for h in range(2):
                square(t + h, t, parts[h])
            for h in range(2):
                high_total(t + h, 1, parts[h])
            for h in range(2):
                std(t + h, parts[h])
            for h in range(2):
                scale_and_shift(t + h, b, parts[h])
            for h in range(2):
                high_x3(t + h, parts[h])
            for h in range(2):
                high_low_rank(t + h, parts[h])
            for h in range(2):
                for m in range(DC):
                    leave_lora(t + h, b, m, parts[h])

        @block.vector
        def _(dve):
            def add_eye(item):
                _, b, c = item
                n = at[item]
                dve.wait_ge(stage_in[n % STAGE_SLOTS], 16 * (n // STAGE_SLOTS + 1))
                part = stage[:, n % STAGE_SLOTS, c * P:(c + 1) * P]
                dve.tensor_tensor(part, part, ident[:, :], ALU.add).then_inc(eye_added, 1)

            def low_plain(item):
                dve.wait_ge(plain_high, plain_at[item] + 1)
                scale, src, high, low, rows = plain_tile(item)
                dve.scalar_tensor_tensor(low[rows], src[rows], scale, high[rows], ALU.mult, ALU.subtract)\
                    .then_inc(tile_done, 1)

            def low_a3(b):
                dve.wait_ge(a3_high, b + 1)
                dve.scalar_tensor_tensor(a3_s[:, b, :, RANK:R2], a3_in[:, b, :, :], A3_SCALE, a3_s[:, b, :, 0:RANK],
                                         ALU.mult, ALU.subtract).then_inc(a3_low, 1)

            def sum_unit(b, u):
                n = 2 * FC * b + u
                slot = at["w", b, u]
                dve.wait_ge(stage_in[slot % STAGE_SLOTS], 16 * (slot // STAGE_SLOTS + 1))
                dve.wait_ge(merge_done, n + 1)
                if n >= SUM_SLOTS:
                    dve.wait_ge(merged_low, n - SUM_SLOTS + 1)
                dve.scalar_tensor_tensor(wsum[:, n % SUM_SLOTS, :], stage[:, slot % STAGE_SLOTS, :],
                                         HIDDEN_SCALE if u % 2 == 0 else WO_SCALE, merge_bank(b, u)[:, :],
                                         ALU.mult, ALU.add).then_inc(tile_done, 1)

            def split_x(s):
                for c in range(DC):
                    dve.wait_ge(x_high, DC * s + c + 1)
                    dve.tensor_tensor(x_l[:, c, :], x_in[:, c, :], x_h[:, c, :], ALU.subtract).then_inc(x_low, 1)

            def leave_layer1(t, m, done, where):
                cols = where[0]
                dve.wait_ge(acc_done, done)
                dve.scalar_tensor_tensor(x2[:, m, cols], acc[m][:, cols], 1.0 / (HIDDEN_SCALE * WO_SCALE),
                                         x1[:, m, cols], ALU.mult, ALU.add).then_inc(x2_full, 1)

            def low_x2(t, m, where):
                cols = where[0]
                dve.wait_ge(x2_high, DC * t + m + 1)
                dve.tensor_tensor(x23_l[:, m, cols], x2[:, m, cols], x23_h[:, m, cols], ALU.subtract)\
                    .then_inc(x2_low, 1)

            def split_x1(s, m, cols):
                dve.wait_ge(x1_full, DC * s + m + 1)
                dve.tensor_copy(x1_h[:, m, cols], x1[:, m, cols]).then_inc(x1_high, 1)
                dve.wait_ge(x1_high, DC * s + m + 1)
                dve.tensor_tensor(x1_l[:, m, cols], x1[:, m, cols], x1_h[:, m, cols], ALU.subtract)\
                    .then_inc(x1_low, 1)

            def low_hidden(s, k, cols):
                slot = k % HIDDEN_SLOTS
                dve.wait_ge(hid_high, FC * s + k + 1)
                dve.scalar_tensor_tensor(hid_l[:, slot, cols], hid[k % 2][:, cols], 0.0, hid_h[:, slot, cols],
                                         ALU.max, ALU.subtract).then_inc(hid_low, 1)

            def adapter_low(t, where):
                cols = where[0]
                dve.wait_ge(up_full, 2 * t + 2)
                dve.tensor_tensor(up_l[:, cols], up[:, cols], up_h[:, cols], ALU.subtract).then_inc(up_low, 1)

            def add_x2(t, m, where):
                cols = where[0]
                dve.wait_ge(adapted, DC * t + m + 1)
                dve.tensor_tensor(y[:, m, cols], y[:, m, cols], x2[:, m, cols], ALU.add).then_inc(y_full, 1)

            def add_chunk(t, n, m, where):
                cols = where[0]
                src, ready = ((y, y_full), (o, squared))[n]
                dve.wait_ge(ready, DC * t + m + 1)
                if m == 1:
                    so_far = src[:, 0, cols]
                else:
                    so_far = total[:, cols]
                    dve.wait_ge(summed[n], 3 * t + m - 1)
                dve.tensor_tensor(total[:, cols], so_far, src[:, m, cols], ALU.add).then_inc(summed[n], 1)

            def low_total(t, n, where):
                cols = where[0]
                dve.wait_ge(total_high[n], t + 1)
                dve.tensor_tensor(total_l[:, cols], total[:, cols], total_h[:, cols], ALU.subtract)\
                    .then_inc(total_low[n], 1)

            def centre(t, where):
                cols, bank = where[:2]
                dve.wait_ge(stat_done[0], t + 1)
                for m in range(DC):
                    dve.tensor_tensor(y[:, m, cols], y[:, m, cols], bank[:, cols], ALU.subtract).then_inc(centred, 1)

            def invert(t, where):
                cols = where[0]
                dve.wait_ge(std_done, t + 1)
                dve.reciprocal(rstd[:, cols], rstd[:, cols]).then_inc(rstd_done, 1)

            def normalise(t, where):
                cols = where[0]
                dve.wait_ge(rstd_done, t + 1)
                for m in range(DC):
                    dve.tensor_tensor(y[:, m, cols], y[:, m, cols], rstd[:, cols], ALU.mult).then_inc(normed, 1)

            def add_x3(t, where):
                cols = where[0]
                for m in range(DC):
                    dve.wait_ge(scaled, DC * t + m + 1)
                    dve.tensor_tensor(y[:, m, cols], y[:, m, cols], x2[:, m, cols], ALU.add).then_inc(x3_full, 1)

            def low_x3(t, where):
                cols = where[0]
                for m in range(DC):
                    dve.wait_ge(x3_high, DC * t + m + 1)
                    dve.tensor_tensor(x23_l[:, m, cols], y[:, m, cols], x23_h[:, m, cols], ALU.subtract)\
                        .then_inc(x3_low, 1)

            def low_low_rank(t, where):
                cols, bank = where[:2]
                dve.wait_ge(low_high, 2 * t + 2)
                dve.tensor_tensor(low_s[R2:2 * R2, cols], bank[0:R2, cols], low_s[0:R2, cols], ALU.subtract)\
                    .then_inc(low_low, 1)

            def add_out(t, m, where):
                cols = where[0]
                dve.wait_ge(out_biased, DC * t + m + 1)
                dve.tensor_tensor(o[:, m, cols], o[:, m, cols], y[:, m, cols], ALU.add).then_inc(out_ready, 1)

            def plain(b, k):
                for item in plan[PER_SEQ * b, k]:
                    if item[0] == "W0":
                        add_eye(item)
                    if item[0] == "B3":
                        low_a3(item[1])
                    if item[0] != "w":
                        low_plain(item)

            def step(s, b, prep, tail=None, cols=whole[0], more=True):
                t = s - 1
                if tail:
                    for m in range(DC):
                        leave_layer1(t, m, DC * t + m + 1, tail)
                    for m in range(DC):
                        low_x2(t, m, tail)
                        if prep:
                            sum_unit(b, m)
                        split_x1(s, m, cols)
                else:
                    sum_unit(b, 0)
                    for m in range(DC):
                        split_x1(s, m, cols)
                    sum_unit(b, 1)
                    sum_unit(b, 2)
                for k in range(FC):
                    if k == 0 and not tail:
                        sum_unit(b, 3)
                    if prep and k < FC - 2:
                        sum_unit(b, 2 * k + 4)
                    low_hidden(s, k, cols)
                    if tail:
                        if k == 0:
                            adapter_low(t, tail)
                        if k in (2, 3):
                            for m in (2 * k - 4, 2 * k - 3):
                                add_x2(t, m, tail)
                                if m:
                                    add_chunk(t, 0, m, tail)
                        if k == 5:
                            centre(t, tail)
                        if k == 6:
                            for m in range(1, DC):
                                add_chunk(t, 1, m, tail)
                        if k in (4, 7):
                            low_total(t, (k - 4) // 3, tail)
                        if k == 8:
                            invert(t, tail)
                        if k == 9:
                            normalise(t, tail)
                        if k == 10:
                            add_x3(t, tail)
                        if k == 11:
                            low_x3(t, tail)
                        if k == 13:
                            low_low_rank(t, tail)
                        if k == 14:
                            add_out(t, 0, tail)
                        if k == 15:
                            for m in range(1, DC):
                                add_out(t, m, tail)
                    if prep and k < FC - 2:
                        sum_unit(b, 2 * k + 5)
                    if prep and (PER_SEQ * b, k) in plan:
                        plain(b, k)
                    if k == 13 and more:
                        split_x(s + 1)

            dve.memset(hid_h[:, 0, :], 0.0).then_inc(warm_set, 1)
            dve.wait_ge(const_set, 4)
            for c, item in enumerate(plan[0, -1][:DC]):
                add_eye(item)
                dve.wait_ge(x_high, c + 1)
                dve.tensor_tensor(x_l[:, c, :], x_in[:, c, :], x_h[:, c, :], ALU.subtract).then_inc(x_low, 1)
                low_plain(item)
            for item in plan[0, -1][DC:2 * DC]:
                low_plain(item)
            step(0, 0, True)
            with dve.Fori(1, PER_SEQ) as s:
                step(s, 0, False, whole)
            step(PER_SEQ, 1, True, whole)
            with dve.Fori(PER_SEQ + 1, GROUPS - 1) as s:
                step(s, 1, False, whole)
            step(GROUPS - 1, 1, False, whole, half[0], False)
            step(GROUPS, 1, False, half, half[0], False)
            t = PASSES - 1
            for h in range(2):
                for m in range(DC):
                    leave_layer1(t + h, m, DC * t + m + 1, parts[h])
            for h in range(2):
                for m in range(DC):
                    low_x2(t + h, m, parts[h])
            for h in range(2):
                adapter_low(t + h, parts[h])
            for h in range(2):
                for m in range(DC):
                    add_x2(t + h, m, parts[h])
                    if m:
                        add_chunk(t + h, 0, m, parts[h])
            for h in range(2):
                low_total(t + h, 0, parts[h])
            for h in range(2):
                centre(t + h, parts[h])
            for h in range(2):
                for m in range(1, DC):
                    add_chunk(t + h, 1, m, parts[h])
            for h in range(2):
                low_total(t + h, 1, parts[h])
            for h in range(2):
                invert(t + h, parts[h])
                normalise(t + h, parts[h])
            for h in range(2):
                add_x3(t + h, parts[h])
            for h in range(2):
                low_x3(t + h, parts[h])
            for h in range(2):
                low_low_rank(t + h, parts[h])
            for h in range(2):
                for m in range(DC):
                    add_out(t + h, m, parts[h])


def kernel(x, itok_B_0_63, itok_B_0_7, itok_B_0_8, itok_B_0_3, L0_cond_W, L0_cond_b, L1_cond_wi, L1_cond_wo,
           L1_cond_common_wi_a, L1_cond_common_wi_b, L1_cond_common_wo_a, L1_cond_common_wo_b,
           L1_cond_experts_wi_a, L1_cond_experts_wi_b, L1_cond_experts_wo_a, L1_cond_experts_wo_b,
           L2_cond_W1, L2_cond_b1, L2_cond_W2, L2_cond_b2, L2_cond_gamma, L2_cond_beta,
           L3_cond_lora_A, L3_cond_lora_B, L3_cond_lang_embed):
    import numpy as np
    from concourse import bacc
    from concourse.bass_utils import run_bass_kernel_spmd

    def lay(a, *order):
        return np.ascontiguousarray(np.transpose(a, order))

    def stacked(common, experts):
        both = [np.concatenate([common, e], axis=0) for e in experts]
        return np.ascontiguousarray(np.stack([np.concatenate([v] * 3, axis=0) for v in both]))

    def columns(v):
        return np.asarray(v).reshape(-1, DC, P).transpose(0, 2, 1)

    x, wi, wo = (np.asarray(v) for v in (x, L1_cond_wi, L1_cond_wo))
    ea, eb, oa, ob = (np.asarray(v) for v in (L1_cond_experts_wi_a, L1_cond_experts_wi_b,
                                              L1_cond_experts_wo_a, L1_cond_experts_wo_b))
    arrays = {
        "x": lay(x.reshape(GROUPS, T, DC, P), 0, 3, 2, 1),
        "ids": np.ascontiguousarray(np.concatenate([np.asarray(v) for v in (
            itok_B_0_63, itok_B_0_7, itok_B_0_8, itok_B_0_3)]).reshape(1, 4 * NB)),
        "w0": np.ascontiguousarray(L0_cond_W),
        "b0": np.ascontiguousarray(columns(L0_cond_b)),
        "wi": lay(wi.reshape(FC, P, DC, P), 0, 3, 2, 1).reshape(FC, P, D),
        "wo": lay(wo, 1, 0).reshape(FC, P, D),
        "wi_a": stacked(np.asarray(L1_cond_common_wi_a), ea),
        "wi_b": stacked(np.asarray(L1_cond_common_wi_b).T, eb.transpose(0, 2, 1)),
        "wo_a": stacked(np.asarray(L1_cond_common_wo_a), oa),
        "wo_b": stacked(np.asarray(L1_cond_common_wo_b).T, ob.transpose(0, 2, 1)),
        "w1": lay(np.asarray(L2_cond_W1).reshape(-1, DC, P, P), 0, 2, 1, 3).reshape(-1, P, D),
        "w2": np.ascontiguousarray(L2_cond_W2),
        "vec2": np.ascontiguousarray(np.concatenate(
            [columns(L2_cond_b2), columns(L2_cond_gamma), columns(L2_cond_beta),
             np.asarray(L2_cond_b1)[:, :, None]], axis=2)),
        "a3": lay(np.asarray(L3_cond_lora_A).reshape(-1, RANK, DC, P), 0, 3, 2, 1),
        "b3": np.ascontiguousarray(np.concatenate([np.asarray(L3_cond_lora_B).transpose(0, 2, 1)] * 6, axis=1)),
        "emb": np.ascontiguousarray(columns(L3_cond_lang_embed)),
    }
    nc = bacc.Bacc("TRN2", target_bir_lowering=False, num_devices=1)
    args = [nc.dram_tensor(name, a.shape, mybir.dt.from_np(a.dtype), kind="ExternalInput").ap()
            for name, a in arrays.items()]
    out = nc.dram_tensor("out", (GROUPS, P, DC, T), F32, kind="ExternalOutput").ap()
    build(nc, *args, out)
    r = run_bass_kernel_spmd(nc, [arrays], core_ids=[0])
    return r.results[0]["out"].transpose(0, 3, 2, 1).reshape(x.shape)
```

```python
from contextlib import ExitStack

import concourse.bass as bass
from concourse import mybir

F32 = mybir.dt.float32
F16 = mybir.dt.float16
I32 = mybir.dt.int32
ALU = mybir.AluOpType
ACT = mybir.ActivationFunctionType

P = 128
D = 512
F = 2048
NB = 2
T = 512
GROUPS = 8
PASSES = GROUPS + 1
HALF = T // 2
QUARTER = T // 4
PER_SEQ = GROUPS // NB
DC = D // P
FC = F // P
RANK = 16
R2 = 2 * RANK
R6 = 3 * R2

W0_SCALE = 64.0
HIDDEN_SCALE = 16.0
WO_SCALE = 64.0
LORA_ALPHA = 2.0
WI_B_SCALE = 4.0
WI_A_SCALE = LORA_ALPHA * HIDDEN_SCALE / WI_B_SCALE
WO_B_SCALE = 4.0
WO_A_SCALE = LORA_ALPHA * WO_SCALE / WO_B_SCALE
W1_SCALE = 32.0
W2_SCALE = 16.0
A3_SCALE = 64.0
B3_SCALE = 64.0
LN_EPS = 1e-5

STAGE_SLOTS = 6
HIDDEN_SLOTS = 3
SUM_SLOTS = 2
WARM_UPS = 20

SMALL_LOADS = 16 * (4 * NB - 1)

B2_AT, GAMMA_AT, BETA_AT, B1_AT, VEC2 = 0, DC, 2 * DC, 3 * DC, 3 * DC + 1


def units_at(k):
    if k < 2:
        return [k + 5], []
    return [2 * k + 3] if k < FC - 1 else [], [2 * k + 4] if k < FC - 2 else []


def staging_plan():
    plan = {(0, -1): [("W0", 0, k) for k in range(DC)]
            + [("WiA", 0, 0), ("WiB", 0, 0), ("WoB", 0, 0), ("WoA", 0, 0)]
            + [("w", 0, u) for u in range(5)]}
    later = [("W1", 0, 0), ("W2", 0, 0), ("B3", 0, 0)] + [("W0", 1, k) for k in range(DC)]
    later += [("WiA", 1, 0), ("WoB", 1, 0)] + [(n, 1, j) for j in range(4) for n in ("WiB", "WoA")]
    later += [("W1", 1, 0), ("W2", 1, 0), ("B3", 1, 0)]
    for k in range(FC):
        plan[0, k] = [("w", 0, u) for place in units_at(k) for u in place]
        if k in (0, 4, 8):
            plan[0, k] += [("WiB", 0, k // 4 + 1), ("WoA", 0, k // 4 + 1)]
        elif k > 1:
            plan[0, k] += later[:2]
            later = later[2:]
    assert not later
    plan[PER_SEQ, -1] = [("w", 1, u) for u in range(5)]
    for k in range(FC):
        plan[PER_SEQ, k] = [("w", 1, u) for place in units_at(k) for u in place]
    return plan


def build(nc, x, ids, w0, b0, wi, wo, wi_a, wi_b, wo_a, wo_b, w1, w2, vec2, a3, b3, emb, out):
    plan = staging_plan()
    order = [item for place in plan.values() for item in place]
    at = {item: n for n, item in enumerate(order)}
    plain = [item for item in order if item[0] != "w"]
    plain_at = {item: n for n, item in enumerate(plain)}

    ctx = ExitStack()
    with ctx:
        def sb(name, shape, dt=F32):
            return ctx.enter_context(nc.sbuf_tensor(name, shape, dt))

        def sem(name):
            return ctx.enter_context(nc.semaphore(name))

        wi_h, wi_l = (sb(f"wi_{p}", [P, FC, DC, P], F16) for p in "hl")
        wo_h, wo_l = (sb(f"wo_{p}", [P, FC, D], F16) for p in "hl")
        w0_h, w0_l = (sb(f"w0_{p}", [P, NB, DC, D], F16) for p in "hl")
        w1_h, w1_l = (sb(f"w1_{p}", [P, NB, DC, P], F16) for p in "hl")
        w2_h, w2_l = (sb(f"w2_{p}", [P, NB, D], F16) for p in "hl")
        wi_a_s = sb("wi_a_s", [R6, NB, D], F16)
        wi_b_s = sb("wi_b_s", [R6, NB, F], F16)
        wo_a_s = sb("wo_a_s", [R6, NB, F], F16)
        wo_b_s = sb("wo_b_s", [R6, NB, D], F16)
        a3_s = sb("a3_s", [P, NB, DC, R2], F16)
        b3_s = sb("b3_s", [R6, NB, D], F16)
        stage = sb("stage", [P, STAGE_SLOTS, D])
        wsum = sb("wsum", [P, SUM_SLOTS, D])
        x_in = sb("x_in", [P, DC, T])
        x_h, x_l = (sb(f"x_{p}", [P, DC, T], F16) for p in "hl")
        x1 = sb("x1", [P, DC, T])
        x1_h, x1_l = (sb(f"x1_{p}", [P, DC, T], F16) for p in "hl")
        hid_h, hid_l = (sb(f"hid_{p}", [P, HIDDEN_SLOTS, T], F16) for p in "hl")
        x2 = sb("x2", [P, DC, T])
        x23_h, x23_l = (sb(f"x23_{p}", [P, DC, T], F16) for p in "hl")
        y = sb("y", [P, DC, T])
        o = sb("o", [P, DC, T])
        up_h, up_l = (sb(f"up_{p}", [P, T], F16) for p in "hl")
        total = sb("total", [P, T])
        up = total
        total_h, total_l = (sb(f"total_{p}", [P, T], F16) for p in "hl")
        rstd = sb("rstd", [P, T])
        low_s = sb("low_s", [R6, T], F16)
        b0_s = sb("b0_s", [P, NB, DC])
        vec2_s = sb("vec2_s", [P, NB, VEC2])
        emb_s = sb("emb_s", [P, NB, DC])
        a3_in = sb("a3_in", [P, NB, DC, RANK])
        ids_s = sb("ids_s", [1, 4 * NB], I32)
        ident = sb("ident", [P, P])
        ones = sb("ones", [P, P], F16)
        eps = sb("eps", [P, 1])

        acc = [ctx.enter_context(nc.psum_tensor(f"acc{m}", [P, T], F32)) for m in range(DC)]
        hid = [ctx.enter_context(nc.psum_tensor(f"hid{m}", [P, T], F32)) for m in range(2)]
        side = ctx.enter_context(nc.psum_tensor("side", [P, T], F32))
        merge = ctx.enter_context(nc.psum_tensor("merge", [P, T], F32))
        l0_bank = [hid[0], hid[1], hid[0], hid[1]]

        whole = (slice(0, T), side, [side])
        half = (slice(0, HALF), side, [side])
        parts = [(slice(0, QUARTER), hid[0], [acc[0], acc[1], side]),
                 (slice(QUARTER, HALF), hid[1], [acc[2], acc[3], merge])]

        def merge_bank(b, u):
            return side if b == 0 and u % 2 else merge

        b0_in = sem("b0_in")
        small_in = sem("small_in")
        x0_in = [sem(f"x0_in{c}") for c in range(DC)]
        x_loaded = sem("x_loaded")
        stage_in = [sem(f"stage_in{n}") for n in range(STAGE_SLOTS)]
        stored = sem("stored")
        l0_done = sem("l0_done")
        hid_done = sem("hid_done")
        chunk_done = sem("chunk_done")
        acc_done = sem("acc_done")
        up_done = sem("up_done")
        down_done = sem("down_done")
        stat_done = [sem(f"stat_done{n}") for n in range(2)]
        low_done = sem("low_done")
        lora_done = sem("lora_done")
        merge_done = sem("merge_done")
        x_high = sem("x_high")
        x1_full = sem("x1_full")
        hid_high = sem("hid_high")
        x2_high = sem("x2_high")
        up_full = sem("up_full")
        y_started = sem("y_started")
        x2_shifted = sem("x2_shifted")
        total_high = [sem(f"total_high{n}") for n in range(2)]
        squared = sem("squared")
        std_done = sem("std_done")
        x3_high = sem("x3_high")
        low_high = sem("low_high")
        out_started = sem("out_started")
        plain_high = sem("plain_high")
        a3_high = sem("a3_high")
        merged_high = sem("merged_high")
        eye_added = sem("eye_added")
        tile_done = sem("tile_done")
        a3_low = sem("a3_low")
        x_low = sem("x_low")
        x1_high = sem("x1_high")
        x1_low = sem("x1_low")
        hid_low = sem("hid_low")
        x2_full = sem("x2_full")
        x2_low = sem("x2_low")
        up_low = sem("up_low")
        y_full = sem("y_full")
        summed = [sem(f"summed{n}") for n in range(2)]
        total_low = [sem(f"total_low{n}") for n in range(2)]
        centred = sem("centred")
        rstd_done = sem("rstd_done")
        normed = sem("normed")
        x3_full = sem("x3_full")
        x3_low = sem("x3_low")
        low_low = sem("low_low")
        out_ready = sem("out_ready")
        const_set = sem("const_set")
        warm_set = sem("warm_set")
        merged_low = sem("merged_low")

        block = ctx.enter_context(nc.Block())

        def plain_tile(item):
            name, b, k = item
            t = slice(k * D, (k + 1) * D)
            src = stage[:, at[item] % STAGE_SLOTS, :]
            if name == "W0":
                return W0_SCALE, src, w0_h[:, b, k, :], w0_l[:, b, k, :], slice(0, P)
            if name == "W1":
                flat = (w[:, b].rearrange("p c a -> p (c a)") for w in (w1_h, w1_l))
                return (W1_SCALE, src, *flat, slice(0, P))
            if name == "W2":
                return W2_SCALE, src, w2_h[:, b, :], w2_l[:, b, :], slice(0, P)
            dst, scale, first = {
                "WiA": (wi_a_s[:, b, :], WI_A_SCALE, 2 * R2), "WiB": (wi_b_s[:, b, t], WI_B_SCALE, R2),
                "WoA": (wo_a_s[:, b, t], WO_A_SCALE, 2 * R2), "WoB": (wo_b_s[:, b, :], WO_B_SCALE, R2),
                "B3": (b3_s[:, b, :], B3_SCALE, 2 * R2)}[name]
            return scale, src[0:R6], dst, dst, slice(first, first + R2)

        @block.sync
        def _(sp):
            sp.dma_start(ids_s[:, :], ids[:, :]).then_inc(stored, 16)
            for c in range(2):
                sp.dma_start(x_in[:, c, :], x[0, :, c, :]).then_inc(x0_in[c], 16)
            sp.wait_ge(stored, 16)

            def chosen(n, rows):
                return [sp.value_load(ids_s[0:1, NB * n + b:NB * n + b + 1], min_val=0, max_val=rows - 1)
                        for b in range(NB)]

            cat = chosen(0, w0.shape[0])

            def load_stage(item):
                name, b, k = item
                t = slice(k * D, (k + 1) * D)
                n = at[item]
                slot = n % STAGE_SLOTS
                rows = P
                if name == "w":
                    src = wi[k // 2] if k % 2 == 0 else wo[k // 2]
                elif name == "W0":
                    src = w0[cat[b], k * P:(k + 1) * P, :]
                elif name == "W1":
                    src = w1[language[b]]
                elif name == "W2":
                    src = w2[language[b]]
                else:
                    rows = R6
                    src = {"WiA": lambda: wi_a[expert[b]], "WiB": lambda: wi_b[expert[b], :, t],
                           "WoA": lambda: wo_a[expert[b], :, t], "WoB": lambda: wo_b[expert[b]],
                           "B3": lambda: b3[lora[b]]}[name]()
                if n >= STAGE_SLOTS:
                    sp.wait_ge(tile_done, n - STAGE_SLOTS + 1)
                sp.dma_start(stage[0:rows, slot, :], src).then_inc(stage_in[slot], 16)

            def load_x(s):
                sp.wait_ge(x_low, DC * s)
                sp.dma_start(x_in[:, :, :], x[s]).then_inc(x_loaded, 16)

            def store(t, group, first, where):
                cols = where[0]
                for m in range(DC):
                    sp.wait_ge(out_ready, DC * t + m + 1)
                    sp.dma_start(out[group, :, m, first:first + cols.stop - cols.start], o[:, m, cols])\
                        .then_inc(stored, 16)

            for item in plan[0, -1][:DC]:
                load_stage(item)
                if item[2] < 2:
                    c = item[2] + 2
                    sp.dma_start(x_in[:, c, :], x[0, :, c, :]).then_inc(x0_in[c], 16)
            sp.dma_start(b0_s[:, 0, :], b0[cat[0]]).then_inc(b0_in, 16)
            expert = chosen(1, wi_a.shape[0])
            for item in plan[0, -1][DC:]:
                load_stage(item)
            language = chosen(2, w1.shape[0])
            lora = chosen(3, a3.shape[0])
            sp.dma_start(b0_s[:, 1, :], b0[cat[1]]).then_inc(small_in, 16)
            for b in range(NB):
                sp.dma_start(vec2_s[:, b, :], vec2[language[b]]).then_inc(small_in, 16)
                sp.dma_start(emb_s[:, b, :], emb[lora[b]]).then_inc(small_in, 16)
                sp.dma_start(a3_in[:, b, :, :], a3[lora[b]]).then_inc(small_in, 16)
            for k in range(FC):
                for item in plan[0, k]:
                    load_stage(item)
                if k == 3:
                    load_x(1)
            with sp.Fori(1, PER_SEQ) as s:
                load_x(s + 1)
                store(s - 1, s - 1, 0, whole)
            for k in range(-1, FC):
                for item in plan[PER_SEQ, k]:
                    load_stage(item)
            load_x(PER_SEQ + 1)
            store(PER_SEQ - 1, PER_SEQ - 1, 0, whole)
            with sp.Fori(PER_SEQ + 1, GROUPS - 1) as s:
                load_x(s + 1)
                store(s - 1, s - 1, 0, whole)
            store(GROUPS - 2, GROUPS - 2, 0, whole)
            store(GROUPS - 1, GROUPS - 1, 0, half)
            for h in range(2):
                store(GROUPS + h, GROUPS - 1, HALF + h * QUARTER, parts[h])
            sp.wait_ge(stored, 16 + 16 * DC * (PASSES + 1))

        @block.gpsimd
        def _(pool):
            pool.memset(ident[:, :], 0.0).then_inc(const_set, 1)
            pool.memset(ones[:, :], 1.0 / D).then_inc(const_set, 1)
            pool.memset(eps[:, :], LN_EPS).then_inc(const_set, 1)
            pool.wait_ge(const_set, 1)
            pool.affine_select(out=ident[:, :], in_=ident[:, :], compare_op=ALU.not_equal, fill=1.0,
                               base=0, pattern=[[-1, P]], channel_multiplier=1).then_inc(const_set, 1)
            for item in order:
                if item[0] == "w":
                    _, b, u = item
                    n = 2 * FC * b + u
                    pool.wait_ge(merged_high, n + 1)
                    src = wsum[:, n % SUM_SLOTS, :]
                    high, low = ((w[:, u // 2].rearrange("p c f -> p (c f)") if u % 2 == 0 else v[:, u // 2, :])
                                 for w, v in ((wi_h, wo_h), (wi_l, wo_l)))
                    pool.tensor_tensor(low, src, high, ALU.subtract).then_inc(merged_low, 1)

        @block.tensor
        def _(pe):
            def three(dst, weights, data, first=True, last=True):
                (wh, wl), (xh, xl) = weights, data
                pe.matmul(dst, wh, xh, start=first, stop=False)
                pe.matmul(dst, wh, xl, start=False, stop=False)
                return pe.matmul(dst, wl, xh, start=False, stop=last)

            def merge_lora(b, u):
                k = u // 2
                before = ("w", b, u - 2 + b)
                if before in at:
                    pe.wait_ge(tile_done, at[before] + 1)
                bank = merge_bank(b, u)
                part = k * P // D
                for item in ([("WiA", b, 0), ("WiB", b, part)] if u % 2 == 0 else [("WoA", b, part), ("WoB", b, 0)]):
                    pe.wait_ge(tile_done, at[item] + 1)
                f = slice(k * P, (k + 1) * P)
                if u % 2 == 0:
                    for c in range(DC):
                        d = slice(c * P, (c + 1) * P)
                        last = pe.matmul(bank[:, d], wi_a_s[:, b, d], wi_b_s[:, b, f], start=True, stop=True)
                else:
                    last = pe.matmul(bank[:, :], wo_a_s[:, b, f], wo_b_s[:, b, :], start=True, stop=True)
                last.then_inc(merge_done, 1)

            def layer0(s, b, m, cols, x_pass, x_cols):
                if m == 0:
                    pe.wait_ge(x_high, DC * x_pass + DC)
                    pe.wait_ge(x_low, DC * x_pass + DC)
                    pe.wait_ge(tile_done, at["W0", b, DC - 1] + 1)
                    pe.wait_ge(hid_low, FC * s)
                if m >= 2:
                    pe.wait_ge(x1_full, DC * s + m - 1)
                d = slice(m * P, (m + 1) * P)
                for c in range(DC):
                    last = three(l0_bank[m][:, cols], (w0_h[:, b, c, d], w0_l[:, b, c, d]),
                                 (x_h[:, c, x_cols], x_l[:, c, x_cols]), c == 0, c == DC - 1)
                last.then_inc(l0_done, 1)

            def first_layer0(b):
                for c in range(DC):
                    pe.wait_ge(x_high, c + 1)
                    pe.wait_ge(x_low, c + 1)
                    pe.wait_ge(tile_done, at["W0", b, c] + 1)
                    for m in range(DC):
                        d = slice(m * P, (m + 1) * P)
                        last = three(acc[m][:, :], (w0_h[:, b, c, d], w0_l[:, b, c, d]),
                                     (x_h[:, c, :], x_l[:, c, :]), c == 0, c == DC - 1)
                        if c == DC - 1:
                            last.then_inc(l0_done, 1)
                    if c == DC - 2:
                        merge_lora(b, 0)
                        merge_lora(b, 1)
                merge_lora(b, 2)

            def adapter_up(t, b, where):
                pe.wait_ge(tile_done, at["W1", b, 0] + 1)
                cols, bank = where[:2]
                for c in range(DC):
                    pe.wait_ge(x2_high, DC * t + c + 1)
                    pe.wait_ge(x2_low, DC * t + c + 1)
                    last = three(bank[:, cols], (w1_h[:, b, c, :], w1_l[:, b, c, :]),
                                 (x23_h[:, c, cols], x23_l[:, c, cols]), c == 0, c == DC - 1)
                last.then_inc(up_done, 1)

            def adapter_down(t, b, m, where):
                if m == 0:
                    pe.wait_ge(up_full, 2 * t + 2)
                    pe.wait_ge(up_low, t + 1)
                    pe.wait_ge(tile_done, at["W2", b, 0] + 1)
                if m >= len(where[2]):
                    pe.wait_ge(y_full, DC * t + m - len(where[2]) + 1)
                d = slice(m * P, (m + 1) * P)
                cols, bank = where[0], where[2][m % len(where[2])]
                three(bank[:, cols], (w2_h[:, b, d], w2_l[:, b, d]), (up_h[:, cols], up_l[:, cols]))\
                    .then_inc(down_done, 1)

            def statistic(t, n, where):
                pe.wait_ge(total_low[n], t + 1)
                cols, bank = where[:2]
                pe.matmul(bank[:, cols], ones[:, :], total_h[:, cols], start=True, stop=False)
                pe.matmul(bank[:, cols], ones[:, :], total_l[:, cols], start=False, stop=True).then_inc(stat_done[n], 1)

            def lora_low(t, b, where):
                pe.wait_ge(a3_low, b + 1)
                cols, bank = where[:2]
                for c in range(DC):
                    pe.wait_ge(x3_high, DC * t + c + 1)
                    pe.wait_ge(x3_low, DC * t + c + 1)
                    pe.matmul(bank[0:R2, cols], a3_s[:, b, c, :], x23_h[:, c, cols], start=c == 0, stop=False)
                    last = pe.matmul(bank[0:R2, cols], a3_s[:, b, c, :], x23_l[:, c, cols], start=False,
                                     stop=c == DC - 1)
                last.then_inc(low_done, 1)

            def lora_up(t, b, m, where):
                if m == 0:
                    pe.wait_ge(low_high, 2 * t + 2)
                    pe.wait_ge(low_low, t + 1)
                    pe.wait_ge(tile_done, at["B3", b, 0] + 1)
                if m >= len(where[2]):
                    pe.wait_ge(out_ready, DC * t + m - len(where[2]) + 1)
                d = slice(m * P, (m + 1) * P)
                cols, bank = where[0], where[2][m % len(where[2])]
                pe.matmul(bank[:, cols], b3_s[:, b, d], low_s[:, cols], start=True, stop=True)\
                    .then_inc(lora_done, 1)

            def first_product(s, b, k, cols, prep):
                if k >= 2:
                    pe.wait_ge(hid_low, FC * s + k - 1)
                if prep:
                    pe.wait_ge(merged_low, 2 * FC * b + 2 * k + 1)
                if k == 0:
                    pe.wait_ge(x1_full, DC * s + DC)
                for c in range(DC):
                    if k == 0:
                        pe.wait_ge(x1_low, DC * s + c + 1)
                    last = three(hid[k % 2][:, cols], (wi_h[:, k, c, :], wi_l[:, k, c, :]),
                                 (x1_h[:, c, cols], x1_l[:, c, cols]), c == 0, c == DC - 1)
                last.then_inc(hid_done, 1)

            def second_product(s, b, k, cols, prep, tail):
                pe.wait_ge(hid_low, FC * s + k + 1)
                if k == 0 and tail:
                    pe.wait_ge(x2_full, DC * s)
                if prep:
                    pe.wait_ge(merged_low, 2 * FC * b + 2 * k + 2)
                slot = k % HIDDEN_SLOTS
                for m in range(DC):
                    d = slice(m * P, (m + 1) * P)
                    last = three(acc[m][:, cols], (wo_h[:, k, d], wo_l[:, k, d]),
                                 (hid_h[:, slot, cols], hid_l[:, slot, cols]), k == 0, k == FC - 1)
                    if k == FC - 1:
                        last.then_inc(acc_done, 1)
                if k < FC - 1:
                    last.then_inc(chunk_done, 1)

            def step(s, b, prep, tail=None, tail_b=None, cols=whole[0], x_pass=None, x_cols=whole[0]):
                t = s - 1
                if tail:
                    for m in range(DC):
                        layer0(s, b, m, cols, s if x_pass is None else x_pass, x_cols)
                        if prep:
                            merge_lora(b, m)
                    adapter_up(t, tail_b, tail)
                    if prep:
                        merge_lora(b, DC)
                else:
                    first_layer0(b)
                for k in range(FC + 2):
                    if k < FC:
                        first_product(s, b, k, cols, prep)
                    if k == 0 and not tail:
                        merge_lora(b, 3)
                        merge_lora(b, 4)
                    if prep:
                        for u in units_at(k)[0]:
                            merge_lora(b, u)
                    if tail:
                        if k in (2, 3):
                            adapter_down(t, tail_b, 2 * (k - 2), tail)
                        if k in (5, 8):
                            statistic(t, (k - 5) // 3, tail)
                        if k == 13:
                            lora_low(t, tail_b, tail)
                        if k in (14, 15):
                            lora_up(t, tail_b, 2 * (k - 14), tail)
                    if k >= 2:
                        second_product(s, b, k - 2, cols, prep, tail)
                    if prep:
                        for u in units_at(k)[1]:
                            merge_lora(b, u)
                    if tail:
                        if k in (2, 3):
                            adapter_down(t, tail_b, 2 * (k - 2) + 1, tail)
                        if k in (14, 15):
                            lora_up(t, tail_b, 2 * (k - 14) + 1, tail)

            pe.wait_ge(warm_set, 1)
            with pe.Fori(0, WARM_UPS // 4):
                for _ in range(4):
                    pe.matmul(side[:, :], hid_h[:, 0, 0:P], hid_h[:, 0, :], start=True, stop=True)
            pe.wait_ge(const_set, 4)
            step(0, 0, True)
            with pe.Fori(1, PER_SEQ) as s:
                step(s, 0, False, whole, 0)
            step(PER_SEQ, 1, True, whole, 0)
            with pe.Fori(PER_SEQ + 1, GROUPS - 1) as s:
                step(s, 1, False, whole, 1)
            step(GROUPS - 1, 1, False, whole, 1, half[0], GROUPS - 1, half[0])
            step(GROUPS, 1, False, half, 1, half[0], GROUPS - 1, slice(HALF, T))
            t, b = PASSES - 1, NB - 1
            for h in range(2):
                adapter_up(t + h, b, parts[h])
            for h in range(2):
                for m in range(DC):
                    adapter_down(t + h, b, m, parts[h])
            for n in range(2):
                for h in range(2):
                    statistic(t + h, n, parts[h])
            lora_low(t, b, parts[0])
            for m in range(DC - 1):
                lora_up(t, b, m, parts[0])
            lora_low(t + 1, b, parts[1])
            lora_up(t, b, DC - 1, parts[0])
            for m in range(DC):
                lora_up(t + 1, b, m, parts[1])

        @block.scalar
        def _(act):
            def high_plain(item):
                n = at[item]
                if item[0] == "W0":
                    act.wait_ge(eye_added, DC * item[1] + item[2] + 1)
                else:
                    act.wait_ge(stage_in[n % STAGE_SLOTS], 16 * (n // STAGE_SLOTS + 1))
                scale, src, high, _, _ = plain_tile(item)
                act.activation(high, src, ACT.Copy, scale=scale).then_inc(plain_high, 1)

            def high_a3(b):
                act.wait_ge(small_in, SMALL_LOADS)
                act.activation(a3_s[:, b, :, 0:RANK], a3_in[:, b, :, :], ACT.Copy, scale=A3_SCALE)\
                    .then_inc(a3_high, 1)

            def high_merged(b, u):
                n = 2 * FC * b + u
                act.wait_ge(tile_done, at["w", b, u] + 1)
                high = wi_h[:, u // 2].rearrange("p c f -> p (c f)") if u % 2 == 0 else wo_h[:, u // 2, :]
                act.activation(high, wsum[:, n % SUM_SLOTS, :], ACT.Copy).then_inc(merged_high, 1)

            def split_x(s):
                act.wait_ge(x_loaded, 16 * s)
                for c in range(DC):
                    act.activation(x_h[:, c, :], x_in[:, c, :], ACT.Copy).then_inc(x_high, 1)

            def high_x2(t, where):
                cols = where[0]
                for m in range(DC):
                    act.wait_ge(x2_full, DC * t + m + 1)
                    act.activation(x23_h[:, m, cols], x2[:, m, cols], ACT.Copy).then_inc(x2_high, 1)

            def leave_layer0(s, b, m, banks, cols):
                act.wait_ge(l0_done, DC * s + m + 1)
                act.activation(x1[:, m, cols], banks[m][:, cols], ACT.Identity, bias=b0_s[:, b, m:m + 1],
                               scale=1.0 / W0_SCALE).then_inc(x1_full, 1)

            def adapter_relu(t, b, where):
                act.wait_ge(up_done, t + 1)
                cols, bank = where[:2]
                for dst in (up, up_h):
                    act.activation(dst[:, cols], bank[:, cols], ACT.Relu, bias=vec2_s[:, b, B1_AT:B1_AT + 1],
                                   scale=1.0 / W1_SCALE).then_inc(up_full, 1)

            def high_hidden(s, k, cols):
                act.wait_ge(hid_done, FC * s + k + 1)
                if k >= HIDDEN_SLOTS:
                    act.wait_ge(chunk_done, (FC - 1) * s + k - HIDDEN_SLOTS + 1)
                act.activation(hid_h[:, k % HIDDEN_SLOTS, cols], hid[k % 2][:, cols], ACT.Relu).then_inc(hid_high, 1)

            def start_y(t, b, where):
                cols = where[0]
                for m in range(DC):
                    act.wait_ge(x2_full, DC * t + m + 1)
                    act.activation(y[:, m, cols], x2[:, m, cols], ACT.Identity,
                                   bias=vec2_s[:, b, B2_AT + m:B2_AT + m + 1]).then_inc(y_started, 1)

            def shift_x2(t, b, where):
                cols = where[0]
                for m in range(DC):
                    act.wait_ge(x2_low, DC * t + m + 1)
                    act.activation(x2[:, m, cols], x2[:, m, cols], ACT.Identity,
                                   bias=vec2_s[:, b, BETA_AT + m:BETA_AT + m + 1]).then_inc(x2_shifted, 1)

            def high_total(t, n, where):
                cols = where[0]
                act.wait_ge(summed[n], 3 * t + 3)
                act.activation(total_h[:, cols], total[:, cols], ACT.Copy).then_inc(total_high[n], 1)

            def square(t, group, where):
                cols = where[0]
                act.wait_ge(stored, 16 + 16 * DC * group)
                for m in range(DC):
                    act.wait_ge(centred, DC * t + m + 1)
                    act.activation(o[:, m, cols], y[:, m, cols], ACT.Square).then_inc(squared, 1)

            def std(t, where):
                cols, bank = where[:2]
                act.wait_ge(stat_done[1], t + 1)
                act.activation(rstd[:, cols], bank[:, cols], ACT.Sqrt, bias=eps[:, :]).then_inc(std_done, 1)

            def high_x3(t, where):
                cols = where[0]
                for m in range(DC):
                    act.wait_ge(x3_full, DC * t + m + 1)
                    act.activation(x23_h[:, m, cols], y[:, m, cols], ACT.Copy).then_inc(x3_high, 1)

            def high_low_rank(t, where):
                cols, bank = where[:2]
                act.wait_ge(low_done, t + 1)
                for first in (0, 2 * R2):
                    act.activation(low_s[first:first + R2, cols], bank[0:R2, cols], ACT.Copy).then_inc(low_high, 1)

            def start_out(t, b, where):
                cols = where[0]
                for m in range(DC):
                    act.wait_ge(x3_low, DC * t + m + 1)
                    act.activation(y[:, m, cols], y[:, m, cols], ACT.Identity, bias=emb_s[:, b, m:m + 1])\
                        .then_inc(out_started, 1)

            def plain(b, k):
                for item in plan[PER_SEQ * b, k]:
                    if item[0] == "B3":
                        high_a3(item[1])
                    if item[0] != "w":
                        high_plain(item)

            def step(s, b, prep, tail=None, tail_b=None, cols=whole[0], more=True):
                t = s - 1
                if tail:
                    high_x2(t, tail)
                    for m in range(DC):
                        leave_layer0(s, b, m, l0_bank, cols)
                        if prep:
                            high_merged(b, m)
                    adapter_relu(t, tail_b, tail)
                    if prep:
                        high_merged(b, DC)
                else:
                    high_merged(b, 0)
                    for m in range(DC):
                        leave_layer0(s, b, m, acc, cols)
                        if m == 0:
                            high_merged(b, 1)
                    high_merged(b, 2)
                for k in range(FC):
                    high_hidden(s, k, cols)
                    if k == 0 and not tail:
                        high_merged(b, 3)
                        high_merged(b, 4)
                    if prep:
                        for u in units_at(k)[0]:
                            high_merged(b, u)
                    if tail:
                        if k == 0:
                            start_y(t, tail_b, tail)
                        if k == 2:
                            shift_x2(t, tail_b, tail)
                        if k in (3, 6):
                            high_total(t, (k - 3) // 3, tail)
                        if k == 5:
                            square(t, t, tail)
                        if k == 8:
                            std(t, tail)
                        if k == 10:
                            high_x3(t, tail)
                        if k == 13:
                            high_low_rank(t, tail)
                        if k == 12:
                            start_out(t, tail_b, tail)
                    if prep:
                        for u in units_at(k)[1]:
                            high_merged(b, u)
                    if prep and (PER_SEQ * b, k) in plan:
                        plain(b, k)
                    if k == 13 and more:
                        split_x(s + 1)

            for c, item in enumerate(plan[0, -1][:DC]):
                act.wait_ge(x0_in[c], 16)
                act.activation(x_h[:, c, :], x_in[:, c, :], ACT.Copy).then_inc(x_high, 1)
                high_plain(item)
            for item in plan[0, -1][DC:2 * DC]:
                high_plain(item)
            act.wait_ge(b0_in, 16)
            act.wait_ge(const_set, 4)
            step(0, 0, True)
            act.wait_ge(small_in, SMALL_LOADS)
            with act.Fori(1, PER_SEQ) as s:
                step(s, 0, False, whole, 0)
            step(PER_SEQ, 1, True, whole, 0)
            with act.Fori(PER_SEQ + 1, GROUPS - 1) as s:
                step(s, 1, False, whole, 1)
            step(GROUPS - 1, 1, False, whole, 1, half[0], False)
            step(GROUPS, 1, False, half, 1, half[0], False)
            t, b = PASSES - 1, NB - 1
            for h in range(2):
                high_x2(t + h, parts[h])
                if h == 0:
                    start_y(t, b, parts[0])
            for h in range(2):
                adapter_relu(t + h, b, parts[h])
            start_y(t + 1, b, parts[1])
            high_total(t, 0, parts[0])
            shift_x2(t, b, parts[0])
            high_total(t + 1, 0, parts[1])
            square(t, t, parts[0])
            square(t + 1, t, parts[1])
            high_total(t, 1, parts[0])
            shift_x2(t + 1, b, parts[1])
            high_total(t + 1, 1, parts[1])
            for h in range(2):
                std(t + h, parts[h])
            high_x3(t, parts[0])
            start_out(t, b, parts[0])
            high_low_rank(t, parts[0])
            high_x3(t + 1, parts[1])
            start_out(t + 1, b, parts[1])
            high_low_rank(t + 1, parts[1])

        @block.vector
        def _(dve):
            def add_eye(item):
                _, b, c = item
                n = at[item]
                dve.wait_ge(stage_in[n % STAGE_SLOTS], 16 * (n // STAGE_SLOTS + 1))
                part = stage[:, n % STAGE_SLOTS, c * P:(c + 1) * P]
                dve.tensor_tensor(part, part, ident[:, :], ALU.add).then_inc(eye_added, 1)

            def low_plain(item):
                dve.wait_ge(plain_high, plain_at[item] + 1)
                scale, src, high, low, rows = plain_tile(item)
                dve.scalar_tensor_tensor(low[rows], src[rows], scale, high[rows], ALU.mult, ALU.subtract)\
                    .then_inc(tile_done, 1)

            def low_a3(b):
                dve.wait_ge(a3_high, b + 1)
                dve.scalar_tensor_tensor(a3_s[:, b, :, RANK:R2], a3_in[:, b, :, :], A3_SCALE, a3_s[:, b, :, 0:RANK],
                                         ALU.mult, ALU.subtract).then_inc(a3_low, 1)

            def sum_unit(b, u):
                n = 2 * FC * b + u
                slot = at["w", b, u]
                dve.wait_ge(stage_in[slot % STAGE_SLOTS], 16 * (slot // STAGE_SLOTS + 1))
                dve.wait_ge(merge_done, n + 1)
                if n >= SUM_SLOTS:
                    dve.wait_ge(merged_low, n - SUM_SLOTS + 1)
                dve.scalar_tensor_tensor(wsum[:, n % SUM_SLOTS, :], stage[:, slot % STAGE_SLOTS, :],
                                         HIDDEN_SCALE if u % 2 == 0 else WO_SCALE, merge_bank(b, u)[:, :],
                                         ALU.mult, ALU.add).then_inc(tile_done, 1)

            def split_x(s):
                for c in range(DC):
                    dve.wait_ge(x_high, DC * s + c + 1)
                    dve.tensor_tensor(x_l[:, c, :], x_in[:, c, :], x_h[:, c, :], ALU.subtract).then_inc(x_low, 1)

            def leave_layer1(t, m, done, where):
                cols = where[0]
                dve.wait_ge(acc_done, done)
                dve.scalar_tensor_tensor(x2[:, m, cols], acc[m][:, cols], 1.0 / (HIDDEN_SCALE * WO_SCALE),
                                         x1[:, m, cols], ALU.mult, ALU.add).then_inc(x2_full, 1)

            def low_x2(t, m, where):
                cols = where[0]
                dve.wait_ge(x2_high, DC * t + m + 1)
                dve.tensor_tensor(x23_l[:, m, cols], x2[:, m, cols], x23_h[:, m, cols], ALU.subtract)\
                    .then_inc(x2_low, 1)

            def split_x1(s, m, cols):
                dve.wait_ge(x1_full, DC * s + m + 1)
                dve.tensor_copy(x1_h[:, m, cols], x1[:, m, cols]).then_inc(x1_high, 1)
                dve.wait_ge(x1_high, DC * s + m + 1)
                dve.tensor_tensor(x1_l[:, m, cols], x1[:, m, cols], x1_h[:, m, cols], ALU.subtract)\
                    .then_inc(x1_low, 1)

            def low_hidden(s, k, cols):
                slot = k % HIDDEN_SLOTS
                dve.wait_ge(hid_high, FC * s + k + 1)
                dve.scalar_tensor_tensor(hid_l[:, slot, cols], hid[k % 2][:, cols], 0.0, hid_h[:, slot, cols],
                                         ALU.max, ALU.subtract).then_inc(hid_low, 1)

            def adapter_low(t, where):
                cols = where[0]
                dve.wait_ge(up_full, 2 * t + 2)
                dve.tensor_tensor(up_l[:, cols], up[:, cols], up_h[:, cols], ALU.subtract).then_inc(up_low, 1)

            def leave_adapter(t, m, where):
                cols, bank = where[0], where[2][m % len(where[2])]
                dve.wait_ge(down_done, DC * t + m + 1)
                dve.wait_ge(y_started, DC * t + m + 1)
                dve.scalar_tensor_tensor(y[:, m, cols], bank[:, cols], 1.0 / W2_SCALE, y[:, m, cols],
                                         ALU.mult, ALU.add).then_inc(y_full, 1)

            def add_chunk(t, n, m, where):
                cols = where[0]
                src, ready = ((y, y_full), (o, squared))[n]
                dve.wait_ge(ready, DC * t + m + 1)
                if m == 1:
                    so_far = src[:, 0, cols]
                else:
                    so_far = total[:, cols]
                    dve.wait_ge(summed[n], 3 * t + m - 1)
                dve.tensor_tensor(total[:, cols], so_far, src[:, m, cols], ALU.add).then_inc(summed[n], 1)

            def low_total(t, n, where):
                cols = where[0]
                dve.wait_ge(total_high[n], t + 1)
                dve.tensor_tensor(total_l[:, cols], total[:, cols], total_h[:, cols], ALU.subtract)\
                    .then_inc(total_low[n], 1)

            def centre(t, m, where):
                cols, bank = where[:2]
                if m == 0:
                    dve.wait_ge(stat_done[0], t + 1)
                dve.tensor_tensor(y[:, m, cols], y[:, m, cols], bank[:, cols], ALU.subtract).then_inc(centred, 1)

            def invert(t, where):
                cols = where[0]
                dve.wait_ge(std_done, t + 1)
                dve.reciprocal(rstd[:, cols], rstd[:, cols]).then_inc(rstd_done, 1)

            def normalise(t, b, m, where):
                cols = where[0]
                if m == 0:
                    dve.wait_ge(rstd_done, t + 1)
                dve.scalar_tensor_tensor(y[:, m, cols], y[:, m, cols], vec2_s[:, b, GAMMA_AT + m:GAMMA_AT + m + 1],
                                         rstd[:, cols], ALU.mult, ALU.mult).then_inc(normed, 1)

            def add_x2(t, m, where):
                cols = where[0]
                dve.wait_ge(normed, DC * t + m + 1)
                dve.wait_ge(x2_shifted, DC * t + m + 1)
                dve.tensor_tensor(y[:, m, cols], y[:, m, cols], x2[:, m, cols], ALU.add).then_inc(x3_full, 1)

            def low_x3(t, m, where):
                cols = where[0]
                dve.wait_ge(x3_high, DC * t + m + 1)
                dve.tensor_tensor(x23_l[:, m, cols], y[:, m, cols], x23_h[:, m, cols], ALU.subtract)\
                    .then_inc(x3_low, 1)

            def low_low_rank(t, where):
                cols, bank = where[:2]
                dve.wait_ge(low_high, 2 * t + 2)
                dve.tensor_tensor(low_s[R2:2 * R2, cols], bank[0:R2, cols], low_s[0:R2, cols], ALU.subtract)\
                    .then_inc(low_low, 1)

            def leave_lora(t, m, where):
                cols, bank = where[0], where[2][m % len(where[2])]
                dve.wait_ge(lora_done, DC * t + m + 1)
                dve.wait_ge(out_started, DC * t + m + 1)
                dve.scalar_tensor_tensor(o[:, m, cols], bank[:, cols], 1.0 / (A3_SCALE * B3_SCALE), y[:, m, cols],
                                         ALU.mult, ALU.add).then_inc(out_ready, 1)

            def plain(b, k):
                for item in plan[PER_SEQ * b, k]:
                    if item[0] == "W0":
                        add_eye(item)
                    if item[0] == "B3":
                        low_a3(item[1])
                    if item[0] != "w":
                        low_plain(item)

            def step(s, b, prep, tail=None, tail_b=None, cols=whole[0], more=True):
                t = s - 1
                if tail:
                    for m in range(DC):
                        leave_layer1(t, m, DC * t + m + 1, tail)
                    for m in range(DC):
                        low_x2(t, m, tail)
                        if prep:
                            sum_unit(b, m)
                        split_x1(s, m, cols)
                    if prep:
                        sum_unit(b, DC)
                else:
                    sum_unit(b, 0)
                    sum_unit(b, 1)
                    for m in range(DC):
                        split_x1(s, m, cols)
                        if m == 1:
                            sum_unit(b, 2)
                for k in range(FC):
                    if k == 0 and not tail:
                        sum_unit(b, 3)
                        sum_unit(b, 4)
                    if prep:
                        for u in units_at(k)[0]:
                            sum_unit(b, u)
                    low_hidden(s, k, cols)
                    if tail:
                        if k == 0:
                            adapter_low(t, tail)
                        if k in (2, 3):
                            for m in (2 * k - 4, 2 * k - 3):
                                leave_adapter(t, m, tail)
                                if m:
                                    add_chunk(t, 0, m, tail)
                        if k == 5:
                            for m in range(DC):
                                centre(t, m, tail)
                        if k == 6:
                            for m in range(1, DC):
                                add_chunk(t, 1, m, tail)
                        if k in (4, 7):
                            low_total(t, (k - 4) // 3, tail)
                        if k == 8:
                            invert(t, tail)
                        if k == 9:
                            for m in range(DC):
                                normalise(t, tail_b, m, tail)
                        if k == 10:
                            for m in range(DC):
                                add_x2(t, m, tail)
                        if k == 11:
                            for m in range(DC):
                                low_x3(t, m, tail)
                        if k == 13:
                            low_low_rank(t, tail)
                        if k in (14, 15):
                            for m in (2 * k - 28, 2 * k - 27):
                                leave_lora(t, m, tail)
                    if prep:
                        for u in units_at(k)[1]:
                            sum_unit(b, u)
                    if prep and (PER_SEQ * b, k) in plan:
                        plain(b, k)
                    if k == 13 and more:
                        split_x(s + 1)

            dve.memset(hid_h[:, 0, :], 0.0).then_inc(warm_set, 1)
            dve.wait_ge(const_set, 4)
            for c, item in enumerate(plan[0, -1][:DC]):
                add_eye(item)
                dve.wait_ge(x_high, c + 1)
                dve.tensor_tensor(x_l[:, c, :], x_in[:, c, :], x_h[:, c, :], ALU.subtract).then_inc(x_low, 1)
                low_plain(item)
            for item in plan[0, -1][DC:2 * DC]:
                low_plain(item)
            step(0, 0, True)
            dve.wait_ge(small_in, SMALL_LOADS)
            with dve.Fori(1, PER_SEQ) as s:
                step(s, 0, False, whole, 0)
            step(PER_SEQ, 1, True, whole, 0)
            with dve.Fori(PER_SEQ + 1, GROUPS - 1) as s:
                step(s, 1, False, whole, 1)
            step(GROUPS - 1, 1, False, whole, 1, half[0], False)
            step(GROUPS, 1, False, half, 1, half[0], False)
            t, b = PASSES - 1, NB - 1
            p, q = parts
            for m in range(DC):
                leave_layer1(t, m, DC * t + m + 1, p)
            for m in range(DC):
                low_x2(t, m, p)
            for m in range(DC):
                leave_layer1(t + 1, m, DC * t + m + 1, q)
            for m in range(DC):
                low_x2(t + 1, m, q)
            adapter_low(t, p)
            for m in range(DC):
                leave_adapter(t, m, p)
                if m == 1:
                    adapter_low(t + 1, q)
                if m > 1:
                    add_chunk(t, 0, m - 1, p)
            for m in range(DC):
                leave_adapter(t + 1, m, q)
                if m == 0:
                    add_chunk(t, 0, DC - 1, p)
                if m == 2:
                    low_total(t, 0, p)
                if m > 1:
                    add_chunk(t + 1, 0, m - 1, q)
            centre(t, 0, p)
            add_chunk(t + 1, 0, DC - 1, q)
            for m in range(1, DC):
                centre(t, m, p)
            low_total(t + 1, 0, q)
            for m in range(1, DC):
                add_chunk(t, 1, m, p)
                if m < DC - 1:
                    centre(t + 1, m - 1, q)
            for m in range(DC - 2, DC):
                centre(t + 1, m, q)
            low_total(t, 1, p)
            for m in range(1, DC):
                add_chunk(t + 1, 1, m, q)
            low_total(t + 1, 1, q)
            invert(t, p)
            for m in range(DC):
                normalise(t, b, m, p)
            for m in range(DC):
                add_x2(t, m, p)
            for m in range(DC):
                low_x3(t, m, p)
            invert(t + 1, q)
            for m in range(DC):
                normalise(t + 1, b, m, q)
            low_low_rank(t, p)
            for m in range(DC):
                add_x2(t + 1, m, q)
            for m in range(DC):
                low_x3(t + 1, m, q)
            for m in range(DC):
                leave_lora(t, m, p)
            low_low_rank(t + 1, q)
            for m in range(DC):
                leave_lora(t + 1, m, q)


def kernel(x, itok_B_0_63, itok_B_0_7, itok_B_0_8, itok_B_0_3, L0_cond_W, L0_cond_b, L1_cond_wi, L1_cond_wo,
           L1_cond_common_wi_a, L1_cond_common_wi_b, L1_cond_common_wo_a, L1_cond_common_wo_b,
           L1_cond_experts_wi_a, L1_cond_experts_wi_b, L1_cond_experts_wo_a, L1_cond_experts_wo_b,
           L2_cond_W1, L2_cond_b1, L2_cond_W2, L2_cond_b2, L2_cond_gamma, L2_cond_beta,
           L3_cond_lora_A, L3_cond_lora_B, L3_cond_lang_embed):
    import numpy as np
    from concourse import bacc
    from concourse.bass_utils import run_bass_kernel_spmd

    def lay(a, *order):
        return np.ascontiguousarray(np.transpose(a, order))

    def stacked(common, experts):
        both = [np.concatenate([common, e], axis=0) for e in experts]
        return np.ascontiguousarray(np.stack([np.concatenate([v] * 3, axis=0) for v in both]))

    def columns(v):
        return np.asarray(v).reshape(-1, DC, P).transpose(0, 2, 1)

    x, wi, wo = (np.asarray(v) for v in (x, L1_cond_wi, L1_cond_wo))
    ea, eb, oa, ob = (np.asarray(v) for v in (L1_cond_experts_wi_a, L1_cond_experts_wi_b,
                                              L1_cond_experts_wo_a, L1_cond_experts_wo_b))
    arrays = {
        "x": lay(x.reshape(GROUPS, T, DC, P), 0, 3, 2, 1),
        "ids": np.ascontiguousarray(np.concatenate([np.asarray(v) for v in (
            itok_B_0_63, itok_B_0_7, itok_B_0_8, itok_B_0_3)]).reshape(1, 4 * NB)),
        "w0": np.ascontiguousarray(L0_cond_W),
        "b0": np.ascontiguousarray(columns(L0_cond_b)),
        "wi": lay(wi.reshape(FC, P, DC, P), 0, 3, 2, 1).reshape(FC, P, D),
        "wo": lay(wo, 1, 0).reshape(FC, P, D),
        "wi_a": stacked(np.asarray(L1_cond_common_wi_a), ea),
        "wi_b": stacked(np.asarray(L1_cond_common_wi_b).T, eb.transpose(0, 2, 1)),
        "wo_a": stacked(np.asarray(L1_cond_common_wo_a), oa),
        "wo_b": stacked(np.asarray(L1_cond_common_wo_b).T, ob.transpose(0, 2, 1)),
        "w1": lay(np.asarray(L2_cond_W1).reshape(-1, DC, P, P), 0, 2, 1, 3).reshape(-1, P, D),
        "w2": np.ascontiguousarray(L2_cond_W2),
        "vec2": np.ascontiguousarray(np.concatenate(
            [columns(L2_cond_b2), columns(L2_cond_gamma), columns(L2_cond_beta),
             np.asarray(L2_cond_b1)[:, :, None]], axis=2)),
        "a3": lay(np.asarray(L3_cond_lora_A).reshape(-1, RANK, DC, P), 0, 3, 2, 1),
        "b3": np.ascontiguousarray(np.concatenate([np.asarray(L3_cond_lora_B).transpose(0, 2, 1)] * 6, axis=1)),
        "emb": np.ascontiguousarray(columns(L3_cond_lang_embed)),
    }
    nc = bacc.Bacc("TRN2", target_bir_lowering=False, num_devices=1)
    args = [nc.dram_tensor(name, a.shape, mybir.dt.from_np(a.dtype), kind="ExternalInput").ap()
            for name, a in arrays.items()]
    out = nc.dram_tensor("out", (GROUPS, P, DC, T), F32, kind="ExternalOutput").ap()
    build(nc, *args, out)
    r = run_bass_kernel_spmd(nc, [arrays], core_ids=[0])
    return r.results[0]["out"].transpose(0, 3, 2, 1).reshape(x.shape)
```
